# Optimizing a Trainium2 kernel written in Bass

```python
import numpy as np
import jax
import jax.numpy as jnp

def _softmax(x, axis=-1):
    return jax.nn.softmax(x, axis=axis)

def _gelu(x):
    return jax.nn.gelu(x, approximate=True)

def _silu(x):
    return jax.nn.silu(x)

def _sigmoid(x):
    return jax.nn.sigmoid(x)

def _layernorm(x, axis=-1, eps=1e-05):
    m = jnp.mean(x, axis=axis, keepdims=True)
    v = jnp.var(x, axis=axis, keepdims=True)
    return (x - m) / jnp.sqrt(v + eps)

def _scatter_add(tgt, idx, src, axis=0):
    return tgt.at[idx].add(src)

def _segment_sum(src, seg, n):
    return jax.ops.segment_sum(src, seg, n)
kernel_name = 'mk_flamingo_gated_d1_seqx_r8_65a035'

def setup_inputs(seed: int=0):
    np.random.seed(seed)
    _w = jnp.asarray

    def _rec_inputs():
        import jax
        import jax.numpy as jnp
        _rk = jax.random.key(seed)
        x = -0.0002928 + 1 * jax.random.normal(jax.random.fold_in(_rk, 1), (4, 512, 128), jnp.float32)
        _lenS = 512 - jax.random.randint(jax.random.fold_in(_rk, 7), (4,), 0, max(1, 512 // 4) + 1, jnp.int32)
        _lenS2 = 77 - jax.random.randint(jax.random.fold_in(_rk, 8), (4,), 0, max(1, 77 // 4) + 1, jnp.int32)
        _ctx_1024P = jax.random.normal(jax.random.fold_in(_rk, 11), (4, 16, 128), jnp.float32)
        _ctx_1024c = jax.random.dirichlet(jax.random.fold_in(_rk, 511), 0.3 * jnp.ones((16,), jnp.float32), (4, 77))
        _ctx_1024t = jnp.einsum('bsk,bkd->bsd', _ctx_1024c, _ctx_1024P)
        _ctx_1024t = _ctx_1024t * jax.lax.rsqrt(jnp.mean(jnp.square(_ctx_1024t)) + 1e-12) * 0.953939
        ctx_1024 = 4.13588e-05 + 0.999923 * (_ctx_1024t + 0.3 * jax.random.normal(jax.random.fold_in(_rk, 611), (4, 77, 128), jnp.float32))
        _g = jax.random.normal(jax.random.fold_in(_rk, 9001), (2, 1), jnp.float32)
        _g = jnp.sign(_g) * jnp.maximum(jnp.abs(_g), 1.0) + (_g == 0) * 1.0
        g_xattn = _g[0]
        g_ffn = _g[1]
        return (x, ctx_1024, g_xattn, g_ffn)
    x, ctx_1024, g_xattn, g_ffn = _rec_inputs()

    def _L0_xattn_setup():
        import jax, jax.numpy as jnp
        import numpy as np
        HIDDEN = 128
        NUM_HEADS = 16
        HEAD_DIM = HIDDEN // NUM_HEADS
        key = jax.random.key(seed)
        k1, k2, k3, k4, k5, k6 = jax.random.split(key, 6)
        B, SQ, SKV = (4, 128, 256)
        s = HIDDEN ** (-0.5)
        return {'xq': jax.random.normal(k1, (B, SQ, HIDDEN), jnp.float32), 'xkv': jax.random.normal(k2, (B, SKV, HIDDEN), jnp.float32), 'Wq': jax.random.normal(k3, (HIDDEN, HIDDEN), jnp.float32) * s, 'Wkv': jax.random.normal(k4, (2 * HIDDEN, HIDDEN), jnp.float32) * s, 'Wout': jax.random.normal(k5, (HIDDEN, HIDDEN), jnp.float32) * s, 'bout': jax.random.normal(k6, (HIDDEN,), jnp.float32) * 0.01}
    _L0_xattn_all = _L0_xattn_setup()
    _L0_xattn_in = {k: v for k, v in _L0_xattn_all.items() if k in ('Wq', 'Wkv', 'Wout', 'bout')}
    del _L0_xattn_all

    def _L0_ffn_setup():
        import jax, jax.numpy as jnp
        import numpy as np
        D_MODEL, D_FF, N_EXPERTS, TOP_K = (128, 512, 8, 2)
        key = jax.random.key(seed)
        k0, k1, k2, k3 = jax.random.split(key, 4)
        x = jax.random.normal(k0, (2, 256, D_MODEL), dtype=jnp.float32)
        Wg = jax.random.normal(k1, (D_MODEL, N_EXPERTS), dtype=jnp.float32) * 0.02
        W1 = jax.random.normal(k2, (N_EXPERTS, D_MODEL, D_FF), dtype=jnp.float32) * 0.02
        b1 = jnp.zeros((N_EXPERTS, D_FF), dtype=jnp.float32)
        W2 = jax.random.normal(k3, (N_EXPERTS, D_FF, D_MODEL), dtype=jnp.float32) * 0.02
        b2 = jnp.zeros((N_EXPERTS, D_MODEL), dtype=jnp.float32)
        return {'x': x, 'Wg': Wg, 'W1': W1, 'b1': b1, 'W2': W2, 'b2': b2}
    _L0_ffn_all = _L0_ffn_setup()
    _L0_ffn_in = {k: v for k, v in _L0_ffn_all.items() if k in ('Wg', 'W1', 'b1', 'W2', 'b2')}
    del _L0_ffn_all
    return {'x': x, 'ctx_1024': ctx_1024, 'g_xattn': g_xattn, 'g_ffn': g_ffn, 'L0_xattn_Wq': _L0_xattn_in['Wq'], 'L0_xattn_Wkv': _L0_xattn_in['Wkv'], 'L0_xattn_Wout': _L0_xattn_in['Wout'], 'L0_xattn_bout': _L0_xattn_in['bout'], 'L0_ffn_Wg': _L0_ffn_in['Wg'], 'L0_ffn_W1': _L0_ffn_in['W1'], 'L0_ffn_b1': _L0_ffn_in['b1'], 'L0_ffn_W2': _L0_ffn_in['W2'], 'L0_ffn_b2': _L0_ffn_in['b2']}

def reference(x, ctx_1024, g_xattn, g_ffn, L0_xattn_Wq, L0_xattn_Wkv, L0_xattn_Wout, L0_xattn_bout, L0_ffn_Wg, L0_ffn_W1, L0_ffn_b1, L0_ffn_W2, L0_ffn_b2):
    import jax
    import jax.numpy as jnp

    def _L0_xattn_ref(xq, xkv, Wq, Wkv, Wout, bout):
        import jax, jax.numpy as jnp
        import numpy as np
        HIDDEN = 128
        NUM_HEADS = 16
        HEAD_DIM = HIDDEN // NUM_HEADS
        B, SQ, H = xq.shape
        SKV = xkv.shape[1]
        scale = HEAD_DIM ** (-0.5)
        q = (xq @ Wq.T).reshape(B, SQ, NUM_HEADS, HEAD_DIM)
        kv = (xkv @ Wkv.T).reshape(B, SKV, 2, NUM_HEADS, HEAD_DIM)
        k, v = (kv[:, :, 0], kv[:, :, 1])
        att = jax.nn.softmax(jnp.einsum('bxhd,byhd->bhxy', q, k) * scale, axis=-1)
        x = jnp.einsum('bhxy,byhd->bxhd', att, v).reshape(B, SQ, H)
        return x @ Wout.T + bout

    def _L0_ffn_ref(x, Wg, W1, b1, W2, b2):
        import jax, jax.numpy as jnp
        import numpy as np
        D_MODEL, D_FF, N_EXPERTS, TOP_K = (128, 512, 8, 2)
        B = x.shape[:-1]
        xs = x.reshape(-1, x.shape[-1])
        T = xs.shape[0]
        gate_logits = xs @ Wg
        weights, sel = jax.lax.top_k(gate_logits, TOP_K)
        weights = jax.nn.softmax(weights.astype(jnp.float32), axis=1).astype(x.dtype)
        h = jax.nn.relu(jnp.einsum('td,edf->etf', xs, W1) + b1[:, None, :])
        out_e = jnp.einsum('etf,efd->etd', h, W2) + b2[:, None, :]
        tok = jnp.arange(T)
        picked = out_e[sel, tok[:, None]]
        out = jnp.einsum('tk,tkd->td', weights, picked)
        return out.reshape(*B, x.shape[-1])
    x = x + jnp.tanh(g_xattn[0]) * _L0_xattn_ref(_layernorm(x, axis=-1), ctx_1024, L0_xattn_Wq, L0_xattn_Wkv, L0_xattn_Wout, L0_xattn_bout)
    x = x + jnp.tanh(g_ffn[0]) * _L0_ffn_ref(_layernorm(x, axis=-1), L0_ffn_Wg, L0_ffn_W1, L0_ffn_b1, L0_ffn_W2, L0_ffn_b2)
    return x

_drawn_inputs = setup_inputs


def setup_inputs(seed=0):
    import zlib

    import numpy as np

    out = dict(_drawn_inputs(seed))
    spreads = {'L0_ffn_b1': (0.0, 0.435), 'L0_ffn_b2': (0.0, 0.1)}
    factors = {'L0_xattn_bout': 5.188}
    for name, (base, spread) in spreads.items():
        noise = np.random.default_rng([zlib.crc32(name.encode()), seed]).standard_normal(out[name].shape)
        drawn = base * np.exp(spread * noise) if base else spread * noise
        out[name] = jnp.asarray(drawn.astype(out[name].dtype))
    for name, factor in factors.items():
        out[name] = (out[name] * factor).astype(out[name].dtype)
    return out
```

```python
from contextlib import ExitStack

import numpy as np

import concourse.bass as bass
from concourse import mybir

P = 128
B, S, D = 4, 512, 128
KEYS, HEADS, HD = 77, 16, 8
T = S // P
TILES = B * T
GRP = 4
UNITS = HEADS // (2 * GRP)
HK = HEADS * KEYS
CH = -(-HK // P)
CROWS = [min(P, HK - P * c) for c in range(CH)]
H0 = [P * c // KEYS for c in range(CH)]
CHEADS = 3
VW = HD + 1
NMIN = 64
PTG = [range(0, 4), range(4, 8), range(8, CH)]

E, F, KF = 8, 512, 4
TOK = B * S
REG = TOK + P
PADROW = E * REG
ROWW = D + 1
NOWHERE = 1 << 20
NT = (2 * TOK + E * (P - 1)) // P
U = 3

_names = [("ident", P), ("upper", P), ("ones", P), ("kmask", HEADS), ("vmask", CH * CHEADS), ("ebase", E),
          ("desc", E), ("le", E * E), ("tile", NT * E), ("tile128", NT)]
CC, _o = {}, 0
for _n, _w in _names:
    CC[_n] = (_o, _o + _w)
    _o += _w
CW = _o


def constants():
    c = np.zeros((P, CW), np.float32)
    put = lambda n, a: c.__setitem__((slice(None), slice(*CC[n])), np.asarray(a, np.float32).reshape(-1, CC[n][1] - CC[n][0]))
    p = np.arange(P)
    put("ident", np.eye(P))
    put("upper", p[:, None] < p[None, :])
    put("ones", np.ones((P, P)))
    put("kmask", p[:, None] // HD == np.arange(HEADS))
    head = (P * np.arange(CH)[None, :, None] + p[:, None, None]) // KEYS
    want = np.array(H0)[None, :, None] + np.arange(CHEADS)
    put("vmask", (head == want) & (head < HEADS))
    put("ebase", np.tile(REG * np.arange(E), (P, 1)))
    put("desc", np.tile(E - np.arange(E), (P, 1)))
    put("le", np.tile((np.arange(E)[None, :] <= np.arange(E)[:, None]).reshape(-1), (P, 1)))
    put("tile", np.tile(np.repeat(np.arange(NT), E), (P, 1)))
    put("tile128", np.tile(P * np.arange(NT), (P, 1)))
    ids = 2 * (P * np.arange(TILES)[None, :, None] + p[:, None, None]) + np.arange(2)
    i = np.concatenate([ids.reshape(P, -1), np.zeros((P, D)), np.full((P, 1), NOWHERE)], 1)
    return c, i.astype(np.int32)


def flamingo(nc, x, ctx, g_x, g_f, wq, wkv, wout, bout, wg, w1, b1, w2, b2, cf, ci, out):
    f32, bf16, i32 = mybir.dt.float32, mybir.dt.bfloat16, mybir.dt.int32
    ALU, ACT, AX = mybir.AluOpType, mybir.ActivationFunctionType, mybir.AxisListType.X
    ds = bass.ds
    st = ExitStack()
    with st:
        sb = lambda n, s, d=f32: st.enter_context(nc.sbuf_tensor(n, s, d))
        pb = lambda n, s, d=f32: st.enter_context(nc.psum_tensor(n, s, d))
        sem = lambda n: st.enter_context(nc.semaphore(n))

        rows_dram = nc.dram_tensor("rows_by_expert", [PADROW + P, ROWW], f32, kind="Internal").ap()
        y_dram = nc.dram_tensor("expert_results", [2 * TOK, D], f32, kind="Internal").ap()

        cst = sb("cst", [P, CW])
        cint = sb("cint", [P, 2 * TILES + ROWW], i32)
        C = lambda n: cst[:, CC[n][0]:CC[n][1]]
        ident = C("ident")
        w_in = sb("w_in", [P, 4, D])
        wT = sb("wT", [P, 3 * D])
        wvT = sb("wvT", [P, D + NMIN])
        wg_sb = sb("wg_sb", [P, NMIN])
        gates = sb("gates", [P, 2])
        tg = sb("tg", [P, 2])
        bo = sb("bo", [P, D])
        tbo = sb("tbo", [P, D])
        w1_sb = sb("w1_sb", [P, E * F])
        w2_sb = sb("w2_sb", [P, KF, E * D])
        b1_bc = sb("b1_bc", [P, E * F])
        b2_bc = sb("b2_bc", [P, E * D])
        x_sb = sb("x_sb", [P, TILES, D])
        xb = sb("xb", [P, TILES, D])
        x1 = sb("x1", [P, TILES, D])
        ctx_sb = sb("ctx_sb", [KEYS, B, D])
        ctxT = sb("ctxT", [P, 3 * KEYS])
        kT = sb("kT", [P, KEYS])
        kblk = sb("kblk", [P, B, HK])
        vblk = sb("vblk", [P, B, CH, NMIN])
        stat1, mv1, rs1 = sb("stat1", [P, T, 6]), sb("mv1", [P, T, 2]), sb("rs1", [P, T])
        stat2, mv2, rs2 = sb("stat2", [P, T, 6]), sb("mv2", [P, T, 2]), sb("rs2", [P, T])
        root = sb("root", [P, 3, T])
        xn = sb("xn", [P, T, D])
        xnT = sb("xnT", [P, S])
        qT = sb("qT", [P, S])
        smax = sb("smax", [P, 2, HEADS])
        dif = sb("dif", [P, 2, HK])
        prob = sb("prob", [P, 2, HK])
        pT = sb("pT", [P, 2, CH * P])
        rsum = sb("rsum", [P, HEADS])
        attn = sb("attn", [P, T, D])
        attnT = sb("attnT", [P, S])
        xs = sb("xs", [P, T, D])
        xsT = sb("xsT", [P, S])
        lg = sb("lg", [P, T, E])
        top = sb("top", [P, 2, T])
        eq = sb("eq", [P, T, E])
        pick = sb("pick", [P, T])
        oh = sb("oh", [P, 2, T, E])
        ohb = sb("ohb", [P, T, E], bf16)
        ohsum = sb("ohsum", [P, T, E])
        carry = sb("carry", [P, E])
        carryb = sb("carryb", [P, E], bf16)
        csum = sb("csum", [P, E])
        upper_b, ones_b = sb("upper_b", [P, P], bf16), sb("ones_b", [P, P], bf16)
        pos = sb("pos", [P, T, E])
        posk = sb("posk", [P, 2, T, E])
        slotf = sb("slotf", [P, 2 * T])
        slot = sb("slot", [P, 2 * T], i32)
        rows = sb("rows", [P, 2, T, ROWW])
        gap = sb("gap", [P, TILES])
        wts = sb("wts", [P, 4, TILES])
        tb = sb("tb", [P, 4, E])
        tbi = sb("tbi", [P, 3, E], i32)
        cmp = sb("cmp", [P, 3, NT * E])
        tj = sb("tj", [P, 4, NT])
        tab = sb("tab", [P, 2, NT], i32)
        xg = sb("xg", [P, U, ROWW])
        xgT = sb("xgT", [P, U, P])
        h1 = sb("h1", [P, U, F])
        hT = sb("hT", [P, U, F])
        yt = sb("yt", [P, U, D])
        dest = sb("dest", [P, U], i32)
        yy = kblk[:].rearrange("p b n -> p (b n)")[:, 0:TILES * 2 * D].rearrange("p (b t d) -> p b t d", b=B, t=T)
        acc, res = xb, x_sb

        sc_ps = pb("sc_ps", [P, 4, 512])
        pt_ps = pb("pt_ps", [P, 2, 512])
        o_ps = pb("o_ps", [P, 512])
        m_ps = pb("m_ps", [P, 512])
        up_ps, ht_ps = sc_ps[:, 0, :], sc_ps[:, 1, :]
        xt_ps, y_ps = pt_ps[:, 0, 0:P], pt_ps[:, 1, 0:D]

        ld_c, ld_w, ld_g, ld_wg, ld_e = (sem(n) for n in ("ld_c", "ld_w", "ld_g", "ld_wg", "ld_e"))
        ld_x = [sem(f"ld_x{b}") for b in range(B)]
        ld_ctx = sem("ld_ctx")
        set_p = sem("set_p")
        tanh_done = sem("tanh_done")
        d = sem("d")
        xn_done = sem("xn_done")
        xs_done = sem("xs_done")
        id_done = sem("id_done")
        m_full = sem("m_full")
        m_read = sem("m_read")
        k_done = sem("k_done")
        xb_done = sem("xb_done")
        sc_full = sem("sc_full")
        sc_read = sem("sc_read")
        pr_done = sem("pr_done")
        pt_full = sem("pt_full")
        pt_read = sem("pt_read")
        pv_done = sem("pv_done")
        o_read = sem("o_read")
        cast_done = sem("cast_done")
        slots_done = sem("slots_done")
        rows_done = sem("rows_done")
        p_step = sem("p_step")
        scat = sem("scat")
        tab_done = sem("tab_done")
        padded = sem("padded")
        x_tile = [sem(f"x_tile{u}") for u in range(U)]
        y_out = [sem(f"y_out{u}") for u in range(U)]
        xt_full, xt_read = sem("xt_full"), sem("xt_read")
        up_full, h_done = sem("up_full"), sem("h_done")
        ht_full, ht_read = sem("ht_full"), sem("ht_read")
        dn_full, y_done = sem("dn_full"), sem("y_done")
        exp_w = sem("exp_w")
        wts_done = sem("wts_done")
        ld_y = [sem(f"ld_y{b}") for b in range(B)]
        res_done = sem("res_done")
        stored = sem("stored")
        block = st.enter_context(nc.Block())

        def tile(i, c):
            return i * U + c, c % U, i + c // U

        PREP = ["ctx", "k", "v", "xn", "q"]
        POST = ["attn", "out", "xs", "logit", "rank"]

        def early(n):
            b, t = divmod(n, T)
            return [("q", b + 1)] if t == T - 1 and b + 1 < B else []

        def late(n):
            b, t = divmod(n, T)
            before = [("ctx",), ("k",), ("v", "xn"), ()][t] if b + 1 < B else ()
            after = [("attn",), ("out",), ("xs",), ("logit", "rank")][t] if b else ()
            return [(s, b + 1) for s in before] + [(s, b - 1) for s in after]

        order = [("w", 0)] + [(s, 0) for s in PREP]
        for n in range(TILES):
            order += early(n) + late(n)
        order += [(s, B - 1) for s in POST]
        M = {s: i + 1 for i, s in enumerate(order + [("count", 0)])}

        @block.sync
        def _(sp):
            sp.dma_start(x_sb[:, 0:T, :], x[0].rearrange("(t p) d -> p t d", p=P)).then_inc(ld_x[0], 16)
            sp.dma_start(cst[:], cf).then_inc(ld_c, 16)
            sp.dma_start(ctx_sb[:], ctx.rearrange("b k d -> k b d")).then_inc(ld_ctx, 16)
            sp.dma_start(wg_sb[:, 0:E], wg).then_inc(ld_wg, 16)
            for b in range(1, B):
                sp.dma_start(x_sb[:, T * b:T * b + T, :], x[b].rearrange("(t p) d -> p t d", p=P)).then_inc(ld_x[b], 16)
            sp.dma_start(w1_sb[:].rearrange("p (e f) -> p e f", e=E), w1.rearrange("e d f -> d e f")).then_inc(ld_e, 16)
            for k in range(KF):
                sp.dma_start(w2_sb[:, k, :].rearrange("p (e d) -> p e d", e=E),
                             w2[:, k * P:k * P + P, :].rearrange("e f d -> f e d")).then_inc(ld_e, 16)
            sp.dma_start(b1_bc[:], b1.rearrange("e f -> (e f)").rearrange("(o n) -> o n", o=1).to_broadcast([P, E * F])).then_inc(ld_e, 16)
            sp.dma_start(b2_bc[:], b2.rearrange("e f -> (e f)").rearrange("(o n) -> o n", o=1).to_broadcast([P, E * D])).then_inc(ld_e, 16)
            pad = cint[:, 2 * TILES:].bitcast(f32)
            sp.wait_ge(ld_c, 32)
            sp.dma_start(rows_dram[PADROW:PADROW + P, :], pad).then_inc(padded, 16)
            sp.wait_ge(tab_done, 1)
            for e in range(E):
                tail = sp.value_load(tbi[0:1, 2, e:e + 1], min_val=REG * e, max_val=REG * e + TOK)
                sp.dma_start(rows_dram[ds(tail, P), :], pad).then_inc(padded, 16)
            sp.wait_ge(padded, 16 * (E + 1))
            sp.wait_ge(scat, 16 * 2 * TILES)

            def load(i, c, first):
                j, u, _ = tile(i, c)
                if not first:
                    sp.wait_ge(xt_full, j - U + 1)
                    sp.wait_ge(id_done, j - U + 1)
                row = sp.value_load(tab[0:1, 1, ds(j, 1)], min_val=0, max_val=PADROW)
                sp.dma_start(xg[:, u, :], rows_dram[ds(row, P), :]).then_inc(x_tile[u], 16)

            for u in range(U):
                load(0, u, True)
            with sp.Fori(0, NT // U - 1) as i:
                for c in range(U, 2 * U):
                    load(i, c, False)
            for u in range(U):
                sp.wait_ge(y_out[u], 16 * (NT // U))
            for b in range(B):
                sp.dma_start(yy[:, b, :, :], y_dram[2 * S * b:2 * S * (b + 1), :]
                             .rearrange("(t p k) d -> p t (k d)", p=P, k=2)).then_inc(ld_y[b], 16)
            for b in range(B):
                sp.wait_ge(res_done, b + 1)
                sp.dma_start(out[b].rearrange("(t p) d -> p t d", p=P), res[:, T * b:T * b + T, :]).then_inc(stored, 16)
            sp.wait_ge(stored, 16 * B)

        @block.tensor
        def _(pe):
            def use(step):
                if M[step] > 1:
                    pe.wait_ge(m_read, M[step] - 1)

            def misc(name, b):
                if name == "rank":
                    pe.wait_ge(cast_done, b + 1)
                    use((name, b))
                    r = m_ps[:, 0:T * E]
                    pe.matmul(r, upper_b[:], ohb[:].rearrange("p t e -> p (t e)"), start=True, stop=False, skip_group_check=True)
                    for k in range(1, T):
                        pe.matmul(r[:, k * E:], ones_b[:], ohb[:, 0:T - k, :].rearrange("p t e -> p (t e)"),
                                  start=False, stop=False, skip_group_check=True)
                    for k in range(T):
                        mm = pe.matmul(r[:, k * E:k * E + E], ones_b[:], carryb[:], start=False, stop=k == T - 1, skip_group_check=True)
                    mm.then_inc(m_full, 1)
                    return
                use((name, b))
                if name == "ctx":
                    if b == 0:
                        pe.wait_ge(ld_ctx, 16)
                    mm = pe.transpose(m_ps[:, 0:KEYS], ctx_sb[:, b, :], ident[0:KEYS, 0:KEYS])
                elif name == "k":
                    mm = pe.matmul(m_ps[:, 0:KEYS], wT[:, D:2 * D], ctxT[:, 0:KEYS], start=True, stop=True)
                elif name == "v":
                    if b == 0:
                        pe.wait_ge(set_p, 3)
                    for c in range(CH):
                        o = P * c % KEYS
                        mm = pe.matmul(m_ps[0:P, c * CHEADS * HD:c * CHEADS * HD + NMIN], ctxT[:, o:o + P],
                                       wvT[:, H0[c] * HD:H0[c] * HD + NMIN], start=True, stop=True, skip_group_check=True)
                elif name in ("xn", "attn", "xs"):
                    if name == "attn":
                        pe.wait_ge(o_read, T * (b + 1))
                    else:
                        pe.wait_ge(xn_done if name == "xn" else xs_done, b + 1)
                    src = {"xn": xn, "attn": attn, "xs": xs}[name]
                    for t in range(T):
                        mm = pe.transpose(m_ps[:, t * P:t * P + P], src[:, t, :], ident)
                elif name == "q":
                    mm = pe.matmul(m_ps[:], wT[:, 0:D], xnT[:], start=True, stop=True)
                elif name == "out":
                    for t in range(T):
                        mm = pe.matmul(m_ps[:, t * P:t * P + P], attnT[:, t * P:t * P + P], wT[:, 2 * D:], start=True, stop=True, skip_group_check=True)
                elif name == "logit":
                    if b == 0:
                        pe.wait_ge(ld_wg, 16)
                    for t in range(T):
                        mm = pe.matmul(m_ps[:, t * NMIN:t * NMIN + NMIN], xsT[:, t * P:t * P + P], wg_sb[:], start=True, stop=True, skip_group_check=True)
                mm.then_inc(m_full, 1)

            def scores(n):
                b, t = divmod(n, T)
                pe.wait_ge(m_read, M["q", b])
                pe.wait_ge(k_done, b + 1)
                for u in range(UNITS):
                    i = n * UNITS + u
                    if i >= 2:
                        pe.wait_ge(sc_read, i - 1)
                    for g in range(2):
                        h = (2 * u + g) * GRP * KEYS
                        mm = pe.matmul(sc_ps[:, 2 * (i % 2) + g, 0:GRP * KEYS], qT[:, t * P:t * P + P],
                                       kblk[:, b, h:h + GRP * KEYS], start=True, stop=True)
                    mm.then_inc(sc_full, 1)

            def values(n):
                b, t = divmod(n, T)
                pe.wait_ge(pr_done, n + 1)
                for g, cs in enumerate(PTG):
                    i = n * len(PTG) + g
                    if i >= 2:
                        pe.wait_ge(pt_read, i - 1)
                    for k, c in enumerate(cs):
                        mm = pe.transpose(pt_ps[0:CROWS[c], i % 2, k * P:k * P + P], prob[:, n % 2, c * P:c * P + CROWS[c]], ident)
                    mm.then_inc(pt_full, 1)
                if n >= 1:
                    pe.wait_ge(o_read, n)
                if t == 0:
                    pe.wait_ge(m_read, M["v", b])
                for g, cs in enumerate(PTG):
                    pe.wait_ge(pt_read, n * len(PTG) + g + 1)
                    for c in cs:
                        mm = pe.matmul(o_ps[:, H0[c] * VW:H0[c] * VW + NMIN], pT[0:CROWS[c], n % 2, c * P:c * P + P],
                                       vblk[0:CROWS[c], b, c, :],
                                       start=c == 0, stop=c == CH - 1, skip_group_check=True)
                mm.then_inc(pv_done, 1)

            pe.wait_ge(ld_c, 32)
            pe.wait_ge(ld_w, 48)
            for k in range(4):
                mm = pe.transpose(m_ps[:, k * D:k * D + D], w_in[:, k, :], ident)
            mm.then_inc(m_full, 1)
            for name in PREP:
                misc(name, 0)
            scores(0)
            for n in range(TILES):
                for step in early(n):
                    misc(*step)
                if n + 1 < TILES:
                    scores(n + 1)
                for step in late(n):
                    misc(*step)
                values(n)
            for name in POST:
                misc(name, B - 1)
            use(("count", 0))
            pe.wait_ge(cast_done, B + 1)
            pe.matmul(m_ps[:, 0:E], ones_b[:], carryb[:], start=True, stop=True).then_inc(m_full, 1)

            def x_turn(i, c):
                j, u, w = tile(i, c)
                pe.wait_ge(x_tile[u], 16 * (w + 1))
                if c:
                    pe.wait_ge(xt_read, j)
                pe.transpose(xt_ps, xg[:, u, 0:D], ident).then_inc(xt_full, 1)

            def up(i, c):
                j, u, w = tile(i, c)
                ex = pe.value_load(tab[0:1, 0, ds(j, 1)], min_val=0, max_val=E - 1)
                pe.wait_ge(xt_read, j + 1)
                if c:
                    pe.wait_ge(h_done, j)
                pe.matmul(up_ps, xgT[:, u, :], w1_sb[:, ds(ex * F, F)], start=True, stop=True).then_inc(up_full, 1)

            def h_turn(i, c):
                j, u, w = tile(i, c)
                pe.wait_ge(h_done, j + 1)
                for k in range(KF):
                    mm = pe.transpose(ht_ps[:, k * P:k * P + P], h1[:, u, k * P:k * P + P], ident)
                mm.then_inc(ht_full, 1)

            def down(i, c):
                j, u, w = tile(i, c)
                ex = pe.value_load(tab[0:1, 0, ds(j, 1)], min_val=0, max_val=E - 1)
                pe.wait_ge(ht_read, j + 1)
                if c:
                    pe.wait_ge(y_done, j)
                for k in range(KF):
                    mm = pe.matmul(y_ps, hT[:, u, k * P:k * P + P], w2_sb[:, k, ds(ex * D, D)], start=k == 0, stop=k == KF - 1)
                mm.then_inc(dn_full, 1)

            def step(i, c, turn=True):
                h_turn(i, c - 1)
                if turn:
                    x_turn(i, c + 1)
                up(i, c)
                down(i, c - 1)

            pe.wait_ge(tab_done, 1)
            pe.wait_ge(ld_e, 16 * (3 + KF))
            x_turn(0, 0)
            x_turn(0, 1)
            up(0, 0)
            step(0, 1)
            with pe.Fori(0, NT // U - 1) as i:
                for c in range(2, 2 + U):
                    step(i, c)
            step(NT // U - 1, 2, turn=False)
            h_turn(NT // U - 1, 2)
            down(NT // U - 1, 2)

        @block.scalar
        def _(act):
            act.dma_start(w_in[:, 0, :], wq).then_inc(ld_w, 16)
            act.dma_start(w_in[:, 1:3, :], wkv.rearrange("(k o) i -> o k i", k=2)).then_inc(ld_w, 16)
            act.dma_start(w_in[:, 3, :], wout).then_inc(ld_w, 16)
            act.dma_start(cint[:], ci).then_inc(ld_c, 16)
            act.dma_start(gates[:, 0:1], g_x.rearrange("(o n) -> o n", o=1).to_broadcast([P, 1])).then_inc(ld_g, 16)
            act.dma_start(gates[:, 1:2], g_f.rearrange("(o n) -> o n", o=1).to_broadcast([P, 1])).then_inc(ld_g, 16)
            act.dma_start(bo[:], bout.rearrange("(o n) -> o n", o=1).to_broadcast([P, D])).then_inc(ld_g, 16)
            act.wait_ge(ld_g, 48)
            act.activation(tg[:], gates[:], ACT.Tanh).then_inc(tanh_done, 1)

            def misc(name, b):
                if name in ("ctx", "out", "v", "logit", "rank"):
                    return
                act.wait_ge(m_full, M[name, b])
                if name == "k":
                    if b:
                        act.wait_ge(k_done, b)
                    act.activation(kT[:], m_ps[:, 0:KEYS], ACT.Copy).then_inc(m_read, 1)
                elif name == "q":
                    if b:
                        act.wait_ge(sc_full, UNITS * T * b)
                    act.activation(qT[:], m_ps[:], ACT.Copy).then_inc(m_read, 1)
                else:
                    dst = {"xn": xnT, "attn": attnT, "xs": xsT}[name]
                    act.activation(dst[:], m_ps[:], ACT.Copy).then_inc(m_read, 1)

            def exps(n):
                act.wait_ge(sc_read, UNITS * (n + 1))
                if n >= 2:
                    act.wait_ge(pt_full, len(PTG) * (n - 1))
                act.activation(prob[:, n % 2, :], dif[:, n % 2, :], ACT.Exp).then_inc(pr_done, 1)

            def evac(n):
                if n >= 2:
                    act.wait_ge(pv_done, n - 1)
                for g, cs in enumerate(PTG):
                    i = n * len(PTG) + g
                    act.wait_ge(pt_full, i + 1)
                    full = [c for c in cs if CROWS[c] == P]
                    w = len(full) * P
                    o = cs[0] * P
                    a = act.activation(pT[:, n % 2, o:o + w], pt_ps[:, i % 2, 0:w], ACT.Copy)
                    if len(full) < len(cs):
                        r = CROWS[-1]
                        a = act.activation(pT[0:r, n % 2, o + w:o + w + P], pt_ps[0:r, i % 2, w:w + P], ACT.Copy)
                    a.then_inc(pt_read, 1)

            for name in PREP:
                misc(name, 0)
            exps(0)
            for n in range(TILES):
                for step in early(n):
                    misc(*step)
                if n + 1 < TILES:
                    exps(n + 1)
                for step in late(n):
                    misc(*step)
                evac(n)
            for name in POST:
                misc(name, B - 1)
            act.wait_ge(slots_done, B)
            act.activation(wts[:, 0, :], gap[:], ACT.Exp).then_inc(exp_w, 1)

            def x_copy(i, c):
                j, u, w = tile(i, c)
                act.wait_ge(xt_full, j + 1)
                if c >= U:
                    act.wait_ge(up_full, j - U + 1)
                act.activation(xgT[:, u, :], xt_ps, ACT.Copy).then_inc(xt_read, 1)

            def relu(i, c):
                j, u, w = tile(i, c)
                act.wait_ge(ht_full, j + 1)
                if c >= U:
                    act.wait_ge(dn_full, j - U + 1)
                act.activation(hT[:, u, :], ht_ps, ACT.Relu).then_inc(ht_read, 1)

            def step(i, c):
                relu(i, c - 1)
                x_copy(i, c + 1)

            x_copy(0, 0)
            x_copy(0, 1)
            for c in range(1, U + 1):
                step(0, c)
            with act.Fori(0, NT // U - 2) as i:
                for c in range(U + 1, 2 * U + 1):
                    step(i, c)
            step(NT // U - 2, U + 1)
            relu(NT // U - 2, U + 1)
            relu(NT // U - 2, U + 2)

        @block.vector
        def _(dve):
            n_d = [0]

            def do(ins):
                n_d[0] += 1
                ins.then_inc(d, 1)
                dve.wait_ge(d, n_d[0])

            def read_m(ins):
                ins.then_inc(m_read, 1)

            def inverse_root(y, var):
                v, h, a = root[:, 0, :], root[:, 1, :], root[:, 2, :]
                do(dve.tensor_scalar(v, var, 1e-5, None, ALU.add))
                dve.tensor_scalar(h, v, -0.5, None, ALU.mult)
                do(dve.tensor_single_scalar(a.bitcast(i32), v.bitcast(i32), 1, ALU.logical_shift_right))
                do(dve.tensor_scalar(y.bitcast(i32), a.bitcast(i32), -1.0, float(0x5F3759DF), ALU.mult, ALU.add))
                for _ in range(3):
                    do(dve.tensor_tensor(a, y, y, ALU.mult))
                    do(dve.tensor_tensor(a, a, h, ALU.mult))
                    do(dve.scalar_tensor_tensor(y, a, 1.5, y, ALU.add, ALU.mult))

            def layernorm(src, stat, mv, rs, dst, signal):
                for t in range(T):
                    last = dve.bn_stats(stat[:, t, :], src[:, t, :])
                do(last)
                for t in range(T):
                    last = dve.bn_aggr(mv[:, t, :], stat[:, t, :])
                do(last)
                inverse_root(rs[:], mv[:, :, 1])
                for t in range(T):
                    last = dve.tensor_scalar(dst[:, t, :], src[:, t, :], mv[:, t, 0:1], rs[:, t:t + 1], ALU.subtract, ALU.mult)
                last.then_inc(signal, 1)

            def ln1(b):
                dve.wait_ge(ld_x[b], 16)
                if b:
                    dve.wait_ge(m_full, M["xn", b - 1])
                layernorm(x_sb[:, T * b:T * b + T, :], stat1, mv1, rs1, xn, xn_done)

            def misc(name, b):
                if name == "ctx":
                    dve.wait_ge(m_full, M[name, b])
                    for k in range(3):
                        last = dve.tensor_copy(ctxT[:, k * KEYS:k * KEYS + KEYS], m_ps[:, 0:KEYS])
                    read_m(last)
                    ln1(b)
                elif name == "v":
                    dve.wait_ge(m_full, M[name, b])
                    v = vblk[:, b, :, 0:CHEADS * VW].rearrange("p c (h w) -> p c h w", w=VW)
                    read_m(dve.tensor_tensor(v[:, :, :, 0:HD], m_ps[:, 0:CH * CHEADS * HD].rearrange("p (c h w) -> p c h w", h=CHEADS, w=HD),
                                             C("vmask").rearrange("p (c h) -> p c h", c=CH).unsqueeze(3).to_broadcast([P, CH, CHEADS, HD]), ALU.mult))
                elif name == "out":
                    dve.wait_ge(m_full, M[name, b])
                    dve.wait_ge(xb_done, b + 1)
                    dve.tensor_tensor(x1[:, T * b:T * b + T, :].rearrange("p t d -> p (t d)"), m_ps[:],
                                      xb[:, T * b:T * b + T, :].rearrange("p t d -> p (t d)"), ALU.add).then_inc(m_read, 1)
                    dve.wait_ge(m_read, M[name, b])
                    if b:
                        dve.wait_ge(m_full, M["xs", b - 1])
                        dve.wait_ge(rows_done, b)
                    layernorm(x1[:, T * b:T * b + T, :], stat2, mv2, rs2, xs, xs_done)
                elif name == "logit":
                    dve.wait_ge(m_full, M[name, b])
                    lgp = m_ps[:, 0:T * NMIN].rearrange("p (t n) -> p t n", n=NMIN)[:, :, 0:E]
                    dve.tensor_copy(lg[:], lgp).then_inc(m_read, 1)
                    dve.wait_ge(m_read, M[name, b])
                    bc = lambda a: a.unsqueeze(2).to_broadcast([P, T, E])
                    desc = C("desc").unsqueeze(1).to_broadcast([P, T, E])
                    for k in range(2):
                        do(dve.tensor_reduce(top[:, k, :], lg[:], AX, ALU.max))
                        do(dve.tensor_tensor(eq[:], lg[:], bc(top[:, k, :]), ALU.is_equal))
                        do(dve.tensor_tensor(eq[:], eq[:], desc, ALU.mult))
                        do(dve.tensor_reduce(pick[:], eq[:], AX, ALU.max))
                        do(dve.tensor_tensor(oh[:, k, :, :], desc, bc(pick[:]), ALU.is_equal))
                        if k == 0:
                            do(dve.scalar_tensor_tensor(lg[:], oh[:, 0, :, :], -3e38, lg[:], ALU.mult, ALU.add))
                    dve.tensor_tensor(gap[:, T * b:T * b + T], top[:, 1, :], top[:, 0, :], ALU.subtract)
                    if b:
                        dve.wait_ge(m_full, M["rank", b - 1])
                    dve.tensor_copy(carryb[:], carry[:])
                    do(dve.tensor_tensor(ohsum[:], oh[:, 0, :, :], oh[:, 1, :, :], ALU.add))
                    dve.tensor_copy(ohb[:], ohsum[:]).then_inc(cast_done, 1)
                    do(dve.tensor_reduce(csum[:], ohsum[:].rearrange("p t e -> p e t"), AX, ALU.add))
                    do(dve.tensor_tensor(carry[:], carry[:], csum[:], ALU.add))
                elif name == "rank":
                    dve.wait_ge(m_full, M[name, b])
                    dve.tensor_tensor(pos[:], m_ps[:, 0:T * E].rearrange("p (t e) -> p t e", e=E),
                                      C("ebase").unsqueeze(1).to_broadcast([P, T, E]), ALU.add).then_inc(m_read, 1)
                    dve.wait_ge(m_read, M[name, b])
                    for k in range(2):
                        last = dve.tensor_tensor(posk[:, k, :, :], oh[:, k, :, :], pos[:], ALU.mult)
                    do(last)
                    do(dve.tensor_reduce(slotf[:], posk[:].rearrange("p k t e -> p (k t) e"), AX, ALU.add))
                    if b:
                        dve.wait_ge(scat, 16 * 2 * T * b)
                    dve.tensor_copy(slot[:], slotf[:]).then_inc(slots_done, 1)

            def softmax(n):
                for u in range(UNITS):
                    i = n * UNITS + u
                    dve.wait_ge(sc_full, i + 1)
                    s = sc_ps[:, 2 * (i % 2):2 * (i % 2) + 2, 0:GRP * KEYS].rearrange("p g (h k) -> p g h k", k=KEYS)
                    m = smax[:, u, 0:2 * GRP].rearrange("p (g h) -> p g h", g=2)
                    do(dve.tensor_reduce(m, s, AX, ALU.max))
                    if u == 0 and n >= 2:
                        dve.wait_ge(pr_done, n - 1)
                    o = dif[:, n % 2, u * 2 * GRP * KEYS:(u + 1) * 2 * GRP * KEYS].rearrange("p (g h k) -> p g h k", g=2, k=KEYS)
                    dve.tensor_tensor(o, s, m.unsqueeze(3).to_broadcast([P, 2, GRP, KEYS]), ALU.subtract).then_inc(sc_read, 1)

            def normalise(n):
                b, t = divmod(n, T)
                dve.wait_ge(pv_done, n + 1)
                if t == 0 and b:
                    dve.wait_ge(m_full, M["attn", b - 1])
                ov = o_ps[:, 0:HEADS * VW].rearrange("p (h w) -> p h w", w=VW)
                do(dve.reciprocal(rsum[:], ov[:, :, HD]))
                dve.tensor_tensor(attn[:, t, :].rearrange("p (h w) -> p h w", w=HD), ov[:, :, 0:HD],
                                  rsum[:].unsqueeze(2).to_broadcast([P, HEADS, HD]), ALU.mult).then_inc(o_read, 1)

            do(dve.memset(carry[:], 0.0))
            ln1(0)
            dve.wait_ge(ld_c, 32)
            dve.tensor_copy(upper_b[:], C("upper"))
            do(dve.tensor_copy(ones_b[:], C("ones")))
            dve.wait_ge(set_p, 3)
            for b in range(B):
                last = dve.tensor_copy(vblk[:, b, :, 0:CHEADS * VW].rearrange("p c (h w) -> p c h w", w=VW)[:, :, :, HD],
                                       C("vmask").rearrange("p (c h) -> p c h", c=CH))
            do(last)
            dve.wait_ge(tanh_done, 1)
            dve.wait_ge(m_full, 1)
            dve.tensor_scalar(wT[:, 0:D], m_ps[:, 0:D], float(HD) ** -0.5, None, ALU.mult)
            dve.tensor_copy(wT[:, D:2 * D], m_ps[:, D:2 * D])
            dve.tensor_copy(wvT[:, 0:D], m_ps[:, 2 * D:3 * D])
            read_m(dve.tensor_scalar(wT[:, 2 * D:], m_ps[:, 3 * D:], tg[:, 0:1], None, ALU.mult))
            dve.wait_ge(m_full, M["ctx", 0])
            for k in range(3):
                last = dve.tensor_copy(ctxT[:, k * KEYS:k * KEYS + KEYS], m_ps[:, 0:KEYS])
            read_m(last)
            misc("v", 0)
            softmax(0)
            for n in range(TILES):
                for step in early(n):
                    misc(*step)
                if n + 1 < TILES:
                    softmax(n + 1)
                for step in late(n):
                    misc(*step)
                normalise(n)
            for name in POST:
                misc(name, B - 1)
            dve.tensor_copy(carryb[:], carry[:]).then_inc(cast_done, 1)
            dve.wait_ge(m_full, M["count", 0])
            cnt = m_ps[:, 0:E]
            dve.tensor_tensor(tbi[:, 2, :], cnt, C("ebase"), ALU.add)
            do(dve.tensor_scalar(tbi[:, 0, :], cnt, float(P - 1), None, ALU.add))
            do(dve.tensor_single_scalar(tbi[:, 1, :], tbi[:, 0, :], 7, ALU.logical_shift_right))
            do(dve.tensor_copy(tb[:, 0, :], tbi[:, 1, :]))
            do(dve.tensor_tensor(cmp[:, 0, 0:E * E].rearrange("p (a b) -> p a b", a=E), C("le").rearrange("p (a b) -> p a b", a=E),
                                 tb[:, 0, :].unsqueeze(1).to_broadcast([P, E, E]), ALU.mult))
            do(dve.tensor_reduce(tb[:, 1, :], cmp[:, 0, 0:E * E].rearrange("p (a b) -> p a b", a=E), AX, ALU.add))
            je = lambda a: a.rearrange("p (j e) -> p j e", e=E)
            jb = lambda a: a.unsqueeze(1).to_broadcast([P, NT, E])
            do(dve.tensor_tensor(je(cmp[:, 1, :]), jb(tb[:, 1, :]), je(C("tile")), ALU.is_le))
            do(dve.tensor_tensor(je(cmp[:, 2, :]), je(cmp[:, 1, :]), jb(tb[:, 0, :]), ALU.mult))
            do(dve.tensor_reduce(tj[:, 0, :], je(cmp[:, 1, :]), AX, ALU.add))
            do(dve.tensor_reduce(tj[:, 1, :], je(cmp[:, 2, :]), AX, ALU.add))
            do(dve.scalar_tensor_tensor(tj[:, 2, :], tj[:, 1, :], -float(P), C("tile128"), ALU.mult, ALU.add))
            do(dve.scalar_tensor_tensor(tj[:, 3, :], tj[:, 0, :], float(REG), tj[:, 2, :], ALU.mult, ALU.add))
            dve.tensor_scalar(tab[:, 1, :], tj[:, 3, :], float(PADROW), None, ALU.min)
            dve.tensor_scalar(tab[:, 0, :], tj[:, 0, :], float(E - 1), None, ALU.min).then_inc(tab_done, 1)
            dve.wait_ge(exp_w, 1)
            do(dve.tensor_scalar(wts[:, 1, :], wts[:, 0, :], 1.0, None, ALU.add))
            do(dve.reciprocal(wts[:, 1, :], wts[:, 1, :]))
            do(dve.tensor_scalar(wts[:, 2, :], wts[:, 1, :], tg[:, 1:2], None, ALU.mult))
            dve.tensor_tensor(wts[:, 3, :], wts[:, 0, :], wts[:, 2, :], ALU.mult).then_inc(wts_done, 1)
            dve.wait_ge(tab_done, 1)
            dve.wait_ge(ld_e, 16 * (3 + KF))

            def hidden(i, c):
                j, u, w = tile(i, c)
                ex = dve.value_load(tab[0:1, 0, ds(j, 1)], min_val=0, max_val=E - 1)
                dve.wait_ge(up_full, j + 1)
                if c >= U:
                    dve.wait_ge(ht_full, j - U + 1)
                dve.tensor_tensor(h1[:, u, :], up_ps, b1_bc[:, ds(ex * F, F)], ALU.add).then_inc(h_done, 1)

            def result(i, c):
                j, u, w = tile(i, c)
                ex = dve.value_load(tab[0:1, 0, ds(j, 1)], min_val=0, max_val=E - 1)
                dve.wait_ge(dn_full, j + 1)
                if c >= U:
                    dve.wait_ge(y_out[u], 16 * w)
                dve.tensor_tensor(yt[:, u, :], y_ps, b2_bc[:, ds(ex * D, D)], ALU.add).then_inc(y_done, 1)

            def step(i, c):
                hidden(i, c)
                result(i, c - 1)

            hidden(0, 0)
            for c in range(1, U + 1):
                step(0, c)
            with dve.Fori(0, NT // U - 2) as i:
                for c in range(U + 1, 2 * U + 1):
                    step(i, c)
            step(NT // U - 2, U + 1)
            step(NT // U - 2, U + 2)
            result(NT // U - 2, U + 2)
            for b in range(B):
                dve.wait_ge(ld_y[b], 16)
                for t in range(T):
                    n = T * b + t
                    last = dve.scalar_tensor_tensor(acc[:, n, :], yy[:, b, t, 0:D], wts[:, 2, n:n + 1], x1[:, n, :], ALU.mult, ALU.add)
                do(last)
                for t in range(T):
                    n = T * b + t
                    last = dve.scalar_tensor_tensor(res[:, n, :], yy[:, b, t, D:2 * D], wts[:, 3, n:n + 1], acc[:, n, :], ALU.mult, ALU.add)
                last.then_inc(res_done, 1)

        @block.gpsimd
        def _(pool):
            pool.memset(wvT[:, D:], 0.0).then_inc(set_p, 1)
            pool.memset(wg_sb[:, E:], 0.0).then_inc(set_p, 1)
            pool.memset(vblk[:], 0.0).then_inc(set_p, 1)
            steps = [0]

            def done(ins):
                steps[0] += 1
                ins.then_inc(p_step, 1)
                pool.wait_ge(p_step, steps[0])

            def k_block(b):
                pool.wait_ge(m_read, M["k", b])
                pool.tensor_tensor(kblk[:, b, :].rearrange("p (h k) -> p h k", k=KEYS), kT[:].unsqueeze(1).to_broadcast([P, HEADS, KEYS]),
                                   C("kmask").unsqueeze(2).to_broadcast([P, HEADS, KEYS]), ALU.mult).then_inc(k_done, 1)

            def with_bias(b):
                pool.wait_ge(ld_x[b], 16)
                pool.tensor_tensor(xb[:, T * b:T * b + T, :], x_sb[:, T * b:T * b + T, :],
                                   tbo[:].unsqueeze(1).to_broadcast([P, T, D]), ALU.add).then_inc(xb_done, 1)

            def send(b):
                pool.wait_ge(xs_done, b + 1)
                if b:
                    pool.wait_ge(scat, 16 * 2 * T * b)
                for k in range(2):
                    pool.tensor_copy(rows[:, k, :, 0:D], xs[:])
                    last = pool.tensor_copy(rows[:, k, :, D:ROWW].bitcast(i32),
                                            cint[:, 2 * T * b:2 * T * b + 2 * T].rearrange("p (t k) -> p t k", k=2)[:, :, k:k + 1])
                last.then_inc(rows_done, 1)
                pool.wait_ge(rows_done, b + 1)
                pool.wait_ge(slots_done, b + 1)
                for k in range(2):
                    for t in range(T):
                        pool.indirect_dma_start(out=rows_dram, out_offset=bass.IndirectOffsetOnAxis(ap=slot[:, k * T + t:k * T + t + 1], axis=0),
                                                in_=rows[:, k, t, :], in_offset=None, bounds_check=PADROW + P - 1, oob_is_err=False).then_inc(scat, 16)

            pool.wait_ge(ld_c, 32)
            pool.wait_ge(tanh_done, 1)
            done(pool.tensor_scalar(tbo[:], bo[:], tg[:, 0:1], None, ALU.mult))
            k_block(0)
            with_bias(0)
            for b in range(1, B):
                k_block(b)
                with_bias(b)
                if b >= 2:
                    send(b - 2)
            send(B - 2)
            send(B - 1)
            pool.wait_ge(tab_done, 1)

            def ids(i, c):
                j, u, w = tile(i, c)
                pool.wait_ge(x_tile[u], 16 * (w + 1))
                if c >= U:
                    pool.wait_ge(y_out[u], 16 * w)
                at = xg[:, u, D:ROWW].bitcast(i32)
                pool.tensor_tensor(dest[:, u:u + 1], at, cint[:, 2 * TILES:2 * TILES + 1], ALU.add).then_inc(id_done, 1)

            def y_send(i, c):
                j, u, w = tile(i, c)
                n = j + 1 if isinstance(i, int) else pool.snap(j + 1)
                pool.wait_ge(id_done, n)
                pool.wait_ge(y_done, n)
                pool.reg_add(bound, last, 1)
                pool.indirect_dma_start(out=y_dram, out_offset=bass.IndirectOffsetOnAxis(ap=dest[:, u:u + 1], axis=0),
                                        in_=yt[:, u, :], in_offset=None, bounds_check=bound, oob_is_err=False).then_inc(y_out[u], 16)

            last, bound = pool.alloc_register("last_result"), pool.alloc_register("bound")
            pool.reg_mov(last, 2 * TOK - 2)
            ids(0, 0)
            for c in range(2):
                ids(0, c + 1)
                y_send(0, c)
            with pool.Fori(0, NT // U - 1) as i:
                for c in range(2, 2 + U):
                    ids(i, c + 1)
                    y_send(i, c)
            y_send(NT // U - 1, 2)


_INS = ["x", "ctx_1024", "g_xattn", "g_ffn", "L0_xattn_Wq", "L0_xattn_Wkv", "L0_xattn_Wout", "L0_xattn_bout",
        "L0_ffn_Wg", "L0_ffn_W1", "L0_ffn_b1", "L0_ffn_W2", "L0_ffn_b2"]
_OUTS = [((B, S, D), "float32")]


def kernel(**inputs):
    import numpy as _np
    import concourse.bacc as _bacc
    from concourse import mybir as _mybir
    from concourse.bass_utils import run_bass_kernel_spmd as _run

    nc = _bacc.Bacc("TRN2", target_bir_lowering=False, num_devices=1)
    arrays, args = {}, []
    given = [(n, _np.ascontiguousarray(inputs[n])) for n in _INS]
    for name, a in given + list(zip(("constants", "integers"), constants())):
        arrays[f"in_{name}_dram"] = a
        args.append(nc.dram_tensor(f"in_{name}_dram", a.shape, _mybir.dt.from_np(a.dtype), kind="ExternalInput").ap())
    for i, (shape, dtype) in enumerate(_OUTS):
        dt = _mybir.dt.from_np(_np.dtype(dtype))
        args.append(nc.dram_tensor(f"out_{i}_dram", shape, dt, kind="ExternalOutput").ap())
    flamingo(nc, *args)
    r = _run(nc, [arrays], core_ids=[0])
    return r.results[0]["out_0_dram"]
```

```python
from contextlib import ExitStack

import numpy as np

import concourse.bass as bass
from concourse import mybir

P = 128
B, S, D = 4, 512, 128
KEYS, HEADS, HD = 77, 16, 8
T = S // P
TILES = B * T
GRP = 4
GROUPS = HEADS // GRP
QD = GRP * HD
UNITS = HEADS // (2 * GRP)
HK = HEADS * KEYS
CH = -(-HK // P)
CROWS = [min(P, HK - P * c) for c in range(CH)]
H0 = [P * c // KEYS for c in range(CH)]
CHEADS = 3
VW = HD + 1
NMIN = 64
PTG = [range(0, 4), range(4, 8), range(8, CH)]

E, F, KF = 8, 512, 4
TOK = B * S
REG = TOK + P
PADROW = E * REG
ROWW = D + 1
NOWHERE = 1 << 20
NT = (2 * TOK + E * (P - 1)) // P
R = 6
U = 3

_names = [("ident", P), ("upper", P), ("ones", P), ("kmask", GRP), ("klow", 1), ("vmask", CH * CHEADS), ("ebase", E),
          ("expert", E), ("le", E * E), ("tile", NT * E), ("tile128", NT)]
CC, _o = {}, 0
for _n, _w in _names:
    CC[_n] = (_o, _o + _w)
    _o += _w
CW = _o


def constants():
    c = np.zeros((P, CW), np.float32)
    put = lambda n, a: c.__setitem__((slice(None), slice(*CC[n])), np.asarray(a, np.float32).reshape(-1, CC[n][1] - CC[n][0]))
    p = np.arange(P)
    put("ident", np.eye(P))
    put("upper", p[:, None] < p[None, :])
    put("ones", np.ones((P, P)))
    put("kmask", p[:, None] % QD // HD == np.arange(GRP))
    put("klow", np.where(p[:, None] >= P // 2, -1, 0))
    head = (P * np.arange(CH)[None, :, None] + p[:, None, None]) // KEYS
    want = np.array(H0)[None, :, None] + np.arange(CHEADS)
    put("vmask", (head == want) & (head < HEADS))
    put("ebase", np.tile(REG * np.arange(E), (P, 1)))
    put("expert", np.tile(np.arange(E), (P, 1)))
    put("le", np.tile((np.arange(E)[None, :] <= np.arange(E)[:, None]).reshape(-1), (P, 1)))
    put("tile", np.tile(np.repeat(np.arange(NT), E), (P, 1)))
    put("tile128", np.tile(P * np.arange(NT), (P, 1)))
    ids = 2 * (P * np.arange(TILES)[None, :, None] + p[:, None, None]) + np.arange(2)
    i = np.concatenate([ids.reshape(P, -1), np.zeros((P, D)), np.full((P, 1), NOWHERE)], 1)
    return c, i.astype(np.int32)


def flamingo(nc, x, ctx, g_x, g_f, wq, wkv, wout, bout, wg, w1, b1, w2, b2, cf, ci, out):
    f32, f32r, bf16, i32 = mybir.dt.float32, mybir.dt.float32r, mybir.dt.bfloat16, mybir.dt.int32
    ALU, ACT, AX = mybir.AluOpType, mybir.ActivationFunctionType, mybir.AxisListType.X
    ds = bass.ds
    PE, DVE = mybir.EngineType.PE, mybir.EngineType.DVE
    st = ExitStack()
    with st:
        sb = lambda n, s, d=f32: st.enter_context(nc.sbuf_tensor(n, s, d))
        pb = lambda n, s, d=f32: st.enter_context(nc.psum_tensor(n, s, d))
        sem = lambda n: st.enter_context(nc.semaphore(n))

        rows_dram = nc.dram_tensor("rows_by_expert", [PADROW + P, ROWW], f32, kind="Internal").ap()
        q_dram = nc.dram_tensor("q_parts_dram", [B, 2, P, S], f32, kind="Internal").ap()
        y_dram = nc.dram_tensor("expert_results", [2 * TOK, D], f32, kind="Internal").ap()

        cst = sb("cst", [P, CW])
        cint = sb("cint", [P, 2 * TILES + ROWW], i32)
        C = lambda n: cst[:, CC[n][0]:CC[n][1]]
        ident = C("ident")
        w_in = sb("w_in", [P, 4, D])
        wT = sb("wT", [P, 2 * D])
        wvT = sb("wvT", [P, D + NMIN])
        wg_sb = sb("wg_sb", [P, NMIN])
        gates = sb("gates", [P, 2])
        tg = sb("tg", [P, 2])
        bo = sb("bo", [P, D])
        tbo = sb("tbo", [P, D])
        w1_sb = sb("w1_sb", [P, E, F + KF])
        w1_now = sb("w1_now", [P, U, F + KF])
        b1_in = sb("b1_in", [E * KF, P])
        w2_sb = sb("w2_sb", [P, E, KF, D])
        b2_bc = sb("b2_bc", [P, E, D])
        x_sb = sb("x_sb", [P, TILES, D])
        xb = sb("xb", [P, TILES, D])
        x1 = sb("x1", [P, TILES, D])
        ctx_sb = sb("ctx_sb", [KEYS, B, D])
        ctxT = sb("ctxT", [P, B, 3, KEYS])
        wk_rep = sb("wk_rep", [P, GROUPS, 4, QD])
        k_high = sb("k_high", [P, GROUPS * KEYS], f32r)
        k_rows = sb("k_rows", [P, GROUPS * KEYS], f32r)
        kblk = sb("kblk", [P, B, HK], f32r)
        q_parts = sb("q_parts", [P, 2, S], f32r)
        q_rows = sb("q_rows", [P, 2, GROUPS, S], f32r)
        vblk = sb("vblk", [P, B, CH, NMIN])
        stat1, mv1, rs1 = sb("stat1", [P, T, 6]), sb("mv1", [P, TILES, 2]), sb("rs1", [P, TILES])
        stat2, mv2, rs2 = sb("stat2", [P, T, 6]), sb("mv2", [P, TILES, 2]), sb("rs2", [P, TILES])
        half1, half2 = sb("half1", [P, TILES]), sb("half2", [P, TILES])
        guess = sb("guess", [P, 2, T])
        newton = sb("newton", [P, T])
        xn = sb("xn", [P, T, D])
        xnT = sb("xnT", [P, S])
        smax = sb("smax", [P, 2, HEADS])
        dif = sb("dif", [P, 2, HK])
        prob = sb("prob", [P, 2, HK])
        pT = sb("pT", [P, 2, CH * P])
        rsum = sb("rsum", [P, HEADS])
        attn = sb("attn", [P, T, D])
        attnT = sb("attnT", [P, S])
        xs = sb("xs", [P, T, D])
        xsT = sb("xsT", [P, S])
        lg = sb("lg", [P, T, E])
        top = sb("top", [P, T, 8])
        topi = sb("topi", [P, T, 8], mybir.dt.uint32)
        topf = sb("topf", [P, 2, T])
        oh = sb("oh", [P, 2, T, E])
        ohb = sb("ohb", [P, T, E], bf16)
        ohsum = sb("ohsum", [P, T, E])
        carry = sb("carry", [P, E])
        carryb = sb("carryb", [P, E], bf16)
        csum = sb("csum", [P, E])
        upper_b, ones_b = sb("upper_b", [P, P], bf16), sb("ones_b", [P, P], bf16)
        pos = sb("pos", [P, T, E])
        posk = sb("posk", [P, 2, T, E])
        slotf = sb("slotf", [P, 2 * T])
        slot = sb("slot", [P, 2 * T], i32)
        rows = sb("rows", [P, 2, T, ROWW])
        gap = sb("gap", [P, TILES])
        wts = sb("wts", [P, 4, TILES])
        tb = sb("tb", [P, 4, E])
        tbi = sb("tbi", [P, 3, E], i32)
        cmp = sb("cmp", [P, 3, NT * E])
        tj = sb("tj", [P, 4, NT])
        first_row = sb("first_row", [P, NT], i32)
        tile_expert = sb("tile_expert", [P, NT], i32)
        xg = sb("xg", [P, R, ROWW])
        xgT = sb("xgT", [P, U, P])
        hT = dif[:].rearrange("p a n -> p (a n)")[:, 0:U * F].rearrange("p (u f) -> p u f", u=U)
        yt = sb("yt", [P, R, D])
        dest = sb("dest", [P, R], i32)
        yy = kblk[:].bitcast(f32).rearrange("p b n -> p (b n)")[:, 0:TILES * 2 * D].rearrange("p (b t d) -> p b t d", b=B, t=T)
        acc, res = xb, x_sb

        sc_ps = pb("sc_ps", [P, 4, 512])
        pt_ps = pb("pt_ps", [P, 2, 512])
        o_ps = pb("o_ps", [P, 512])
        m_ps = pb("m_ps", [P, 512])
        up_ps = sc_ps[:, 0:U, :]
        xt_ps, y_ps = pt_ps[:, 0, 0:P], pt_ps[:, 1, 0:D]

        ld_id, ld_c, ld_w, ld_g, ld_wg, ld_e = (sem(n) for n in ("ld_id", "ld_c", "ld_w", "ld_g", "ld_wg", "ld_e"))
        ld_b1 = sem("ld_b1")
        w1_ready = sem("w1_ready")
        wout_done = sem("wout_done")
        counts_done = sem("counts_done")
        ld_x = [sem(f"ld_x{b}") for b in range(B)]
        ld_ctx = sem("ld_ctx")
        q_high = sem("q_high")
        k_hi = sem("k_hi")
        q_out = sem("q_out")
        q_in = [sem("q_in0"), sem("q_in1")]
        root1, root2 = sem("root1"), sem("root2")
        seed1, seed2 = sem("seed1"), sem("seed2")
        set_p = sem("set_p")
        tanh_done = sem("tanh_done")
        d = sem("d")
        xn_done = sem("xn_done")
        xs_done = sem("xs_done")
        id_done = sem("id_done")
        m_full = sem("m_full")
        m_read = sem("m_read")
        k_done = sem("k_done")
        xb_done = sem("xb_done")
        sc_full = sem("sc_full")
        sc_read = sem("sc_read")
        pr_done = sem("pr_done")
        pt_full = sem("pt_full")
        pt_read = sem("pt_read")
        pv_done = sem("pv_done")
        o_read = sem("o_read")
        cast_done = sem("cast_done")
        slots_done = sem("slots_done")
        rows_done = sem("rows_done")
        p_step = sem("p_step")
        scat = sem("scat")
        tab_done = sem("tab_done")
        padded = sem("padded")
        x_tile = [sem(f"x_tile{r}") for r in range(R)]
        y_out = [sem(f"y_out{r}") for r in range(R)]
        xt_full, xt_read = sem("xt_full"), sem("xt_read")
        up_full, h_done = sem("up_full"), sem("h_done")
        dn_full, y_done = sem("dn_full"), sem("y_done")
        exp_w = sem("exp_w")
        wts_done = sem("wts_done")
        ld_y = [sem(f"ld_y{b}") for b in range(B)]
        res_done = sem("res_done")
        stored = sem("stored")
        block = st.enter_context(nc.Block())

        def load_experts(engine, i, c, n):
            _, v = nc.values_load_multi_w_load_instructions(
                tile_expert[0:1, ds(i * R + c, n)], engines=[engine], min_val=0, max_val=E - 1,
                skip_runtime_bounds_check_because="the table holds experts alone")
            return v

        def tile(i, c):
            return i * R + c, c % U, c % R, i + c // R

        PREP = ["xn", "q", "k", "v"]
        POST = ["attn", "out", "norm2", "xs", "logit", "route", "rank"]
        PLACE = {(0, 0): [("attn", -1)], (0, 1): [("xn", 1), ("norm1", 2)], (0, 2): [("q", 1)],
                 (1, 1): [("k", 1)], (1, 2): [("out", -1)],
                 (2, 1): [("v", 1), ("norm2", -1)], (2, 2): [("xs", -1)],
                 (3, 0): [("logit", -1)], (3, 1): [("route", -1)], (3, 2): [("rank", -1)]}

        def slot_steps(n, k):
            b, t = divmod(n, T)
            return [(s, b + at) for s, at in PLACE.get((t, k), []) if 0 <= b + at < B]

        order = [("w", 0), ("ctx", 0), ("b1", 0)] + [(s, 0) for s in PREP]
        for n in range(TILES):
            for k in range(3):
                order += slot_steps(n, k)
        order += [(s, B - 1) for s in POST]
        M = {s: i + 1 for i, s in enumerate(s for s in order + [("count", 0)] if s[0] not in ("norm1", "norm2", "route"))}

        def tail(queue, e):
            row = queue.value_load(tbi[0:1, 2, e:e + 1], min_val=REG * e, max_val=REG * e + TOK)
            queue.dma_start(rows_dram[ds(row, P), :], cint[:, 2 * TILES:].bitcast(f32)).then_inc(padded, 16)

        @block.sync
        def _(sp):
            sp.dma_start(x_sb[:, 0:T, :], x[0].rearrange("(t p) d -> p t d", p=P)).then_inc(ld_x[0], 16)
            sp.dma_start(ident, cf[:, 0:P]).then_inc(ld_id, 16)
            sp.dma_start(cst[:, P:], cf[:, P:]).then_inc(ld_c, 16)
            sp.dma_start(ctx_sb[:], ctx.rearrange("b k d -> k b d")).then_inc(ld_ctx, 16)
            sp.dma_start(wg_sb[:, 0:E], wg).then_inc(ld_wg, 16)
            sp.dma_start(b1_in[:], b1.rearrange("e (k p) -> (e k) p", k=KF)).then_inc(ld_b1, 16)
            for b in range(1, B):
                sp.dma_start(x_sb[:, T * b:T * b + T, :], x[b].rearrange("(t p) d -> p t d", p=P)).then_inc(ld_x[b], 16)

            def spread_q(b):
                sp.wait_ge(m_read, M["q", b])
                sp.dma_start(q_dram[b].rearrange("h p s -> p h s"), q_parts[:].bitcast(f32)).then_inc(q_out, 16)
                sp.wait_ge(q_out, 16 * (b + 1))
                if b >= 2:
                    sp.wait_ge(sc_full, UNITS * T * (b - 1))
                for k in range(4):
                    sp.dma_start(q_rows[QD * k:QD * k + QD, b % 2, :, :].bitcast(f32),
                                 q_dram[b, k % 2].rearrange("(g r) s -> r g s", r=QD)).then_inc(q_in[b % 2], 16)

            spread_q(0)
            sp.dma_start(w1_sb[:, :, 0:F], w1.rearrange("e d f -> d e f")).then_inc(ld_e, 16)
            for k in range(KF):
                sp.dma_start(w2_sb[:, :, k, :], w2[:, k * P:k * P + P, :].rearrange("e f d -> f e d")).then_inc(ld_e, 16)
            sp.dma_start(b2_bc[:].rearrange("p e d -> p (e d)"), b2.rearrange("e f -> (e f)").rearrange("(o n) -> o n", o=1).to_broadcast([P, E * D])).then_inc(ld_e, 16)
            for b in range(1, B):
                spread_q(b)
            pad = cint[:, 2 * TILES:].bitcast(f32)
            sp.wait_ge(ld_c, 32)
            sp.dma_start(rows_dram[PADROW:PADROW + P, :], pad).then_inc(padded, 16)
            sp.wait_ge(counts_done, 1)
            for e in range(0, E, 2):
                tail(sp, e)
            sp.wait_ge(tab_done, 1)
            sp.wait_ge(padded, 16 * (E + 1))
            sp.wait_ge(scat, 16 * 2 * TILES)

            def load(i, c):
                j, _, r, _ = tile(i, c)
                if c >= R:
                    sp.wait_ge(xt_full, j - R + 1)
                    sp.wait_ge(id_done, j - R + 1)
                row = sp.value_load(first_row[0:1, ds(j, 1)], min_val=0, max_val=PADROW)
                sp.dma_start(xg[:, r, :], rows_dram[ds(row, P), :]).then_inc(x_tile[r], 16)

            for c in range(R):
                load(0, c)
            with sp.Fori(0, NT // R - 1) as i:
                for c in range(R, 2 * R):
                    load(i, c)
            for c in range(R, R + NT % R):
                load(NT // R - 1, c)
            for r in range(R):
                sp.wait_ge(y_out[r], 16 * len(range(r, NT, R)))
            for b in range(B):
                sp.dma_start(yy[:, b, :, :], y_dram[2 * S * b:2 * S * (b + 1), :]
                             .rearrange("(t p k) d -> p t (k d)", p=P, k=2)).then_inc(ld_y[b], 16)
            for b in range(B):
                sp.wait_ge(res_done, b + 1)
                sp.dma_start(out[b].rearrange("(t p) d -> p t d", p=P), res[:, T * b:T * b + T, :]).then_inc(stored, 16)
            sp.wait_ge(stored, 16 * B)

        @block.tensor
        def _(pe):
            def use(step):
                if M[step] > 1:
                    pe.wait_ge(m_read, M[step] - 1)

            def misc(name, b):
                if name in ("norm1", "norm2", "route"):
                    return
                if name == "rank":
                    pe.wait_ge(cast_done, b + 1)
                    use((name, b))
                    r = m_ps[:, 0:T * E]
                    pe.matmul(r, upper_b[:], ohb[:].rearrange("p t e -> p (t e)"), start=True, stop=False, skip_group_check=True)
                    for k in range(1, T):
                        pe.matmul(r[:, k * E:], ones_b[:], ohb[:, 0:T - k, :].rearrange("p t e -> p (t e)"),
                                  start=False, stop=False, skip_group_check=True)
                    for k in range(T):
                        mm = pe.matmul(r[:, k * E:k * E + E], ones_b[:], carryb[:], start=False, stop=k == T - 1, skip_group_check=True)
                    mm.then_inc(m_full, 1)
                    return
                use((name, b))
                if name == "ctx":
                    pe.wait_ge(ld_ctx, 16)
                    for k in range(B):
                        mm = pe.transpose(m_ps[:, k * KEYS:k * KEYS + KEYS], ctx_sb[:, k, :], ident[0:KEYS, 0:KEYS])
                elif name == "b1":
                    pe.wait_ge(ld_b1, 16)
                    mm = pe.transpose(m_ps[:, 0:E * KF], b1_in[:], ident[0:E * KF, 0:E * KF])
                elif name == "k":
                    for g in range(GROUPS):
                        mm = pe.matmul(m_ps[:, g * KEYS:g * KEYS + KEYS], wk_rep[:, g, :, :].rearrange("p a b -> p (a b)"),
                                       ctxT[:, b, 0, :], start=True, stop=True, skip_group_check=True)
                elif name == "v":
                    if b == 0:
                        pe.wait_ge(set_p, 3)
                    for c in range(CH):
                        o = P * c % KEYS
                        mm = pe.matmul(m_ps[0:P, c * CHEADS * HD:c * CHEADS * HD + NMIN], ctxT[:, b, :, :].rearrange("p r k -> p (r k)")[:, o:o + P],
                                       wvT[:, H0[c] * HD:H0[c] * HD + NMIN], start=True, stop=True, skip_group_check=True)
                elif name in ("xn", "attn", "xs"):
                    if name == "attn":
                        pe.wait_ge(o_read, T * (b + 1))
                    else:
                        pe.wait_ge(xn_done if name == "xn" else xs_done, b + 1)
                    src = {"xn": xn, "attn": attn, "xs": xs}[name]
                    for t in range(T):
                        mm = pe.transpose(m_ps[:, t * P:t * P + P], src[:, t, :], ident)
                elif name == "q":
                    mm = pe.matmul(m_ps[:], wT[:, 0:D], xnT[:], start=True, stop=True)
                elif name == "out":
                    if b == 0:
                        pe.wait_ge(wout_done, 1)
                    for t in range(T):
                        mm = pe.matmul(m_ps[:, t * P:t * P + P], attnT[:, t * P:t * P + P], wT[:, D:], start=True, stop=True, skip_group_check=True)
                elif name == "logit":
                    if b == 0:
                        pe.wait_ge(ld_wg, 16)
                    for t in range(T):
                        mm = pe.matmul(m_ps[:, t * NMIN:t * NMIN + NMIN], xsT[:, t * P:t * P + P], wg_sb[:], start=True, stop=True, skip_group_check=True)
                mm.then_inc(m_full, 1)

            def scores(n):
                b, t = divmod(n, T)
                if t == 0:
                    pe.wait_ge(q_in[b % 2], 16 * 4 * (b // 2 + 1))
                    pe.wait_ge(k_done, b + 1)
                for u in range(UNITS):
                    i = n * UNITS + u
                    if i >= 2:
                        pe.wait_ge(sc_read, i - 1)
                    for g in range(2):
                        h = (2 * u + g) * GRP * KEYS
                        mm = pe.matmul(sc_ps[:, 2 * (i % 2) + g, 0:GRP * KEYS], q_rows[:, b % 2, 2 * u + g, t * P:t * P + P],
                                       kblk[:, b, h:h + GRP * KEYS], start=True, stop=True)
                    mm.then_inc(sc_full, 1)

            def turn_probs(n):
                pe.wait_ge(pr_done, n + 1)
                for g, cs in enumerate(PTG):
                    i = n * len(PTG) + g
                    if i >= 2:
                        pe.wait_ge(pt_read, i - 1)
                    for k, c in enumerate(cs):
                        mm = pe.transpose(pt_ps[0:CROWS[c], i % 2, k * P:k * P + P], prob[:, n % 2, c * P:c * P + CROWS[c]], ident)
                    mm.then_inc(pt_full, 1)

            def values(n):
                b, t = divmod(n, T)
                if n >= 1:
                    pe.wait_ge(o_read, n)
                if t == 0:
                    pe.wait_ge(m_read, M["v", b])
                for g, cs in enumerate(PTG):
                    pe.wait_ge(pt_read, n * len(PTG) + g + 1)
                    for c in cs:
                        mm = pe.matmul(o_ps[:, H0[c] * VW:H0[c] * VW + NMIN], pT[0:CROWS[c], n % 2, c * P:c * P + P],
                                       vblk[0:CROWS[c], b, c, :],
                                       start=c == 0, stop=c == CH - 1, skip_group_check=True)
                mm.then_inc(pv_done, 1)

            pe.wait_ge(ld_id, 16)
            pe.wait_ge(ld_w, 48)
            for k in range(4):
                mm = pe.transpose(m_ps[:, k * D:k * D + D], w_in[:, k, :], ident)
            mm.then_inc(m_full, 1)
            for name in ["ctx", "b1"] + PREP:
                misc(name, 0)
            scores(0)
            def slot_of(n, k):
                for step in slot_steps(n, k):
                    misc(*step)

            for n in range(TILES):
                if n + 1 < TILES:
                    scores(n + 1)
                slot_of(n, 0)
                turn_probs(n)
                slot_of(n, 1)
                values(n)
                slot_of(n, 2)
            for name in POST:
                misc(name, B - 1)
            use(("count", 0))
            pe.wait_ge(cast_done, B + 1)
            pe.matmul(m_ps[:, 0:E], ones_b[:], carryb[:], start=True, stop=True).then_inc(m_full, 1)

            def x_turn(i, c):
                j, u, r, w = tile(i, c)
                pe.wait_ge(x_tile[r], 16 * (w + 1))
                if c:
                    pe.wait_ge(xt_read, j)
                pe.transpose(xt_ps, xg[:, r, 0:D], ident).then_inc(xt_full, 1)

            def up(i, c):
                j, u, r, w = tile(i, c)
                pe.wait_ge(xt_read, j + 1)
                pe.wait_ge(w1_ready, j + 1)
                if c >= U:
                    pe.wait_ge(h_done, j - U + 1)
                for k in range(KF):
                    mm = pe.matmul(up_ps[:, u, k * P:k * P + P], w1_now[:, u, k * P:k * P + P], xgT[:, u, :],
                                   start=True, stop=True, skip_group_check=True)
                mm.then_inc(up_full, 1)

            def down(i, c, ex):
                j, u, r, w = tile(i, c)
                pe.wait_ge(h_done, j + 1)
                if c:
                    pe.wait_ge(y_done, j)
                for k in range(KF):
                    mm = pe.matmul(y_ps, hT[:, u, k * P:k * P + P], w2_sb[:, ds(ex, 1), k, :], start=k == 0, stop=k == KF - 1)
                mm.then_inc(dn_full, 1)

            def step(i, c, ex, turn=True):
                if turn:
                    x_turn(i, c + 1)
                up(i, c)
                down(i, c - 1, ex)

            pe.wait_ge(tab_done, 1)
            pe.wait_ge(ld_e, 16 * (2 + KF))
            x_turn(0, 0)
            x_turn(0, 1)
            up(0, 0)
            ex = load_experts(PE, 0, 0, 1)
            step(0, 1, ex[0])
            with pe.Fori(0, NT // R) as i:
                x_turn(i, 3)
                up(i, 2)
                ex = load_experts(PE, i, 1, R)
                down(i, 1, ex[0])
                for c in range(3, 2 + R):
                    step(i, c, ex[c - 2])
            i = NT // R
            ex = load_experts(PE, i, 1, 2)
            step(i, 2, ex[0], turn=False)
            down(i, 2, ex[1])

        @block.scalar
        def _(act):
            act.dma_start(w_in[:, 0, :], wq).then_inc(ld_w, 16)
            act.dma_start(w_in[:, 1:3, :], wkv.rearrange("(k o) i -> o k i", k=2)).then_inc(ld_w, 16)
            act.dma_start(w_in[:, 3, :], wout).then_inc(ld_w, 16)
            act.dma_start(cint[:], ci).then_inc(ld_c, 16)
            act.dma_start(gates[:, 0:1], g_x.rearrange("(o n) -> o n", o=1).to_broadcast([P, 1])).then_inc(ld_g, 16)
            act.dma_start(gates[:, 1:2], g_f.rearrange("(o n) -> o n", o=1).to_broadcast([P, 1])).then_inc(ld_g, 16)
            act.dma_start(bo[:], bout.rearrange("(o n) -> o n", o=1).to_broadcast([P, D])).then_inc(ld_g, 16)
            act.wait_ge(ld_g, 48)
            act.activation(tg[:], gates[:], ACT.Tanh).then_inc(tanh_done, 1)

            def misc(name, b):
                if name not in ("k", "q", "xn", "attn", "xs", "logit"):
                    return
                act.wait_ge(m_full, M[name, b])
                if name == "k":
                    if b:
                        act.wait_ge(m_read, M["k", b - 1])
                    act.activation(k_high[:], m_ps[:, 0:GROUPS * KEYS], ACT.Copy).then_inc(k_hi, 1)
                elif name == "q":
                    if b:
                        act.wait_ge(q_out, 16 * b)
                    act.activation(q_parts[:, 0, :], m_ps[:], ACT.Copy).then_inc(q_high, 1)
                elif name == "logit":
                    if b:
                        act.wait_ge(slots_done, b)
                    act.activation(lg[:], m_ps[:, 0:T * NMIN].rearrange("p (t n) -> p t n", n=NMIN)[:, :, 0:E], ACT.Copy).then_inc(m_read, 1)
                else:
                    dst = {"xn": xnT, "attn": attnT, "xs": xsT}[name]
                    act.activation(dst[:], m_ps[:], ACT.Copy).then_inc(m_read, 1)

            def exps(n):
                act.wait_ge(sc_read, UNITS * (n + 1))
                if n >= 2:
                    act.wait_ge(pt_full, len(PTG) * (n - 1))
                act.activation(prob[:, n % 2, :], dif[:, n % 2, :], ACT.Exp).then_inc(pr_done, 1)

            def evac(n):
                if n >= 2:
                    act.wait_ge(pv_done, n - 1)
                for g, cs in enumerate(PTG):
                    i = n * len(PTG) + g
                    act.wait_ge(pt_full, i + 1)
                    full = [c for c in cs if CROWS[c] == P]
                    w = len(full) * P
                    o = cs[0] * P
                    a = act.activation(pT[:, n % 2, o:o + w], pt_ps[:, i % 2, 0:w], ACT.Copy)
                    if len(full) < len(cs):
                        r = CROWS[-1]
                        a = act.activation(pT[0:r, n % 2, o + w:o + w + P], pt_ps[0:r, i % 2, w:w + P], ACT.Copy)
                    a.then_inc(pt_read, 1)

            for name in PREP:
                misc(name, 0)
            exps(0)
            def slot_of(n, k):
                for step in slot_steps(n, k):
                    misc(*step)

            for n in range(TILES):
                slot_of(n, 0)
                evac(n)
                slot_of(n, 1)
                if n + 1 < TILES:
                    exps(n + 1)
                slot_of(n, 2)
            for name in POST:
                misc(name, B - 1)
            act.wait_ge(counts_done, 1)
            for e in range(1, E, 2):
                tail(act, e)
            act.activation(wts[:, 0, :], gap[:], ACT.Exp).then_inc(exp_w, 1)

            def x_copy(i, c):
                j, u, r, w = tile(i, c)
                act.wait_ge(xt_full, j + 1)
                if c >= U:
                    act.wait_ge(up_full, j - U + 1)
                act.activation(xgT[:, u, :], xt_ps, ACT.Copy).then_inc(xt_read, 1)

            def relu(i, c):
                j, u, r, w = tile(i, c)
                act.wait_ge(up_full, j + 1)
                if c >= U:
                    act.wait_ge(dn_full, j - U + 1)
                for k in range(KF):
                    a = act.activation(hT[:, u, k * P:k * P + P], up_ps[:, u, k * P:k * P + P], ACT.Relu,
                                       bias=w1_now[:, u, F + k:F + k + 1])
                a.then_inc(h_done, 1)

            def step(i, c):
                x_copy(i, c + 1)
                relu(i, c)

            x_copy(0, 0)
            for c in range(U):
                step(0, c)
            with act.Fori(0, NT // R - 1) as i:
                for c in range(U, U + R):
                    step(i, c)
            i = NT // R - 1
            for c in range(U, NT - R * i - 1):
                step(i, c)
            relu(i, NT - R * i - 1)

        @block.vector
        def _(dve):
            n_d = [0]

            def do(ins):
                n_d[0] += 1
                ins.then_inc(d, 1)
                dve.wait_ge(d, n_d[0])

            def read_m(ins):
                ins.then_inc(m_read, 1)

            def stats(src, stat, mv, half, rs, seeded):
                for t in range(T):
                    last = dve.bn_stats(stat[:, t, :], src[:, t, :])
                do(last)
                for t in range(T):
                    last = dve.bn_aggr(mv[:, t, :], stat[:, t, :])
                do(last)
                v, a = guess[:, 0, :], guess[:, 1, :]
                dve.tensor_scalar(half, mv[:, :, 1], 1e-5, -0.5, ALU.add, ALU.mult)
                do(dve.tensor_scalar(v, mv[:, :, 1], 1e-5, None, ALU.add))
                do(dve.tensor_single_scalar(a.bitcast(i32), v.bitcast(i32), 1, ALU.logical_shift_right))
                dve.tensor_scalar(rs.bitcast(i32), a.bitcast(i32), -1.0, float(0x5F3759DF), ALU.mult, ALU.add).then_inc(seeded, 1)

            def normalised(dst, src, mv, rs, signal):
                for t in range(T):
                    last = dve.tensor_scalar(dst[:, t, :], src[:, t, :], mv[:, t, 0:1], rs[:, t:t + 1], ALU.subtract, ALU.mult)
                last.then_inc(signal, 1)

            def bt(a, b):
                return a[:, T * b:T * b + T]

            def stats1(b):
                dve.wait_ge(ld_x[b], 16)
                if b:
                    dve.wait_ge(seed1, b)
                stats(bt(x_sb, b), stat1, bt(mv1, b), bt(half1, b), bt(rs1, b), seed1)

            def misc(name, b):
                if name == "ctx":
                    dve.wait_ge(m_full, M[name, b])
                    for k in range(3):
                        last = dve.tensor_copy(ctxT[:, :, k, :], m_ps[:, 0:B * KEYS].rearrange("p (b k) -> p b k", k=KEYS))
                    read_m(last)
                elif name == "norm1":
                    dve.wait_ge(root1, b + 1)
                    if b:
                        dve.wait_ge(m_full, M["xn", b - 1])
                    normalised(xn, bt(x_sb, b), bt(mv1, b), bt(rs1, b), xn_done)
                elif name == "k":
                    dve.wait_ge(k_hi, b + 1)
                    if b:
                        dve.wait_ge(k_done, b)
                    dve.scalar_tensor_tensor(k_rows[:], k_high[:].bitcast(f32), C("klow"), m_ps[:, 0:GROUPS * KEYS],
                                             ALU.mult, ALU.add).then_inc(m_read, 1)
                elif name == "q":
                    dve.wait_ge(q_high, b + 1)
                    dve.tensor_tensor(q_parts[:, 1, :], m_ps[:], q_parts[:, 0, :].bitcast(f32), ALU.subtract).then_inc(m_read, 1)
                elif name == "v":
                    dve.wait_ge(m_full, M[name, b])
                    v = vblk[:, b, :, 0:CHEADS * VW].rearrange("p c (h w) -> p c h w", w=VW)
                    read_m(dve.tensor_tensor(v[:, :, :, 0:HD], m_ps[:, 0:CH * CHEADS * HD].rearrange("p (c h w) -> p c h w", h=CHEADS, w=HD),
                                             C("vmask").rearrange("p (c h) -> p c h", c=CH).unsqueeze(3).to_broadcast([P, CH, CHEADS, HD]), ALU.mult))
                elif name == "out":
                    dve.wait_ge(m_full, M[name, b])
                    dve.wait_ge(xb_done, b + 1)
                    dve.tensor_tensor(x1[:, T * b:T * b + T, :].rearrange("p t d -> p (t d)"), m_ps[:],
                                      xb[:, T * b:T * b + T, :].rearrange("p t d -> p (t d)"), ALU.add).then_inc(m_read, 1)
                    dve.wait_ge(m_read, M[name, b])
                    if b:
                        dve.wait_ge(seed2, b)
                    stats(bt(x1, b), stat2, bt(mv2, b), bt(half2, b), bt(rs2, b), seed2)
                elif name == "norm2":
                    dve.wait_ge(root2, b + 1)
                    if b:
                        dve.wait_ge(m_full, M["xs", b - 1])
                        dve.wait_ge(rows_done, b)
                    normalised(xs, bt(x1, b), bt(mv2, b), bt(rs2, b), xs_done)
                elif name == "route":
                    dve.wait_ge(m_read, M["logit", b])
                    for t in range(T):
                        last = dve.max(top[:, t, :], lg[:, t, :])
                    do(last)
                    for t in range(T):
                        last = dve.max_index(topi[:, t, :], top[:, t, :], lg[:, t, :])
                    do(last)
                    do(dve.tensor_copy(topf[:], topi[:, :, 0:2].rearrange("p t k -> p k t")))
                    dve.tensor_tensor(bt(gap, b), top[:, :, 1], top[:, :, 0], ALU.subtract)
                    for k in range(2):
                        last = dve.tensor_tensor(oh[:, k, :, :], C("expert").unsqueeze(1).to_broadcast([P, T, E]),
                                                 topf[:, k, :].unsqueeze(2).to_broadcast([P, T, E]), ALU.is_equal)
                    do(last)
                    if b:
                        dve.wait_ge(m_full, M["rank", b - 1])
                    dve.tensor_copy(carryb[:], carry[:])
                    do(dve.tensor_tensor(ohsum[:], oh[:, 0, :, :], oh[:, 1, :, :], ALU.add))
                    dve.tensor_copy(ohb[:], ohsum[:]).then_inc(cast_done, 1)
                    do(dve.tensor_reduce(csum[:], ohsum[:].rearrange("p t e -> p e t"), AX, ALU.add))
                    do(dve.tensor_tensor(carry[:], carry[:], csum[:], ALU.add))
                elif name == "rank":
                    dve.wait_ge(m_full, M[name, b])
                    dve.tensor_tensor(pos[:], m_ps[:, 0:T * E].rearrange("p (t e) -> p t e", e=E),
                                      C("ebase").unsqueeze(1).to_broadcast([P, T, E]), ALU.add).then_inc(m_read, 1)
                    dve.wait_ge(m_read, M[name, b])
                    for k in range(2):
                        last = dve.tensor_tensor(posk[:, k, :, :], oh[:, k, :, :], pos[:], ALU.mult)
                    do(last)
                    do(dve.tensor_reduce(slotf[:], posk[:].rearrange("p k t e -> p (k t) e"), AX, ALU.add))
                    if b:
                        dve.wait_ge(scat, 16 * 2 * T * b)
                    dve.tensor_copy(slot[:], slotf[:]).then_inc(slots_done, 1)

            def softmax(n):
                for u in range(UNITS):
                    i = n * UNITS + u
                    dve.wait_ge(sc_full, i + 1)
                    s = sc_ps[:, 2 * (i % 2):2 * (i % 2) + 2, 0:GRP * KEYS].rearrange("p g (h k) -> p g h k", k=KEYS)
                    m = smax[:, u, 0:2 * GRP].rearrange("p (g h) -> p g h", g=2)
                    do(dve.tensor_reduce(m, s, AX, ALU.max))
                    if u == 0 and n >= 2:
                        dve.wait_ge(pr_done, n - 1)
                    o = dif[:, n % 2, u * 2 * GRP * KEYS:(u + 1) * 2 * GRP * KEYS].rearrange("p (g h k) -> p g h k", g=2, k=KEYS)
                    dve.tensor_tensor(o, s, m.unsqueeze(3).to_broadcast([P, 2, GRP, KEYS]), ALU.subtract).then_inc(sc_read, 1)

            def normalise(n):
                b, t = divmod(n, T)
                dve.wait_ge(pv_done, n + 1)
                if t == 0 and b:
                    dve.wait_ge(m_full, M["attn", b - 1])
                ov = o_ps[:, 0:HEADS * VW].rearrange("p (h w) -> p h w", w=VW)
                do(dve.reciprocal(rsum[:], ov[:, :, HD]))
                dve.tensor_tensor(attn[:, t, :].rearrange("p (h w) -> p h w", w=HD), ov[:, :, 0:HD],
                                  rsum[:].unsqueeze(2).to_broadcast([P, HEADS, HD]), ALU.mult).then_inc(o_read, 1)

            do(dve.memset(carry[:], 0.0))
            stats1(0)
            dve.wait_ge(m_full, 1)
            dve.tensor_scalar(wT[:, 0:D], m_ps[:, 0:D], float(HD) ** -0.5, None, ALU.mult)
            dve.tensor_copy(wk_rep[:], m_ps[:, D:2 * D].rearrange("p (g r) -> p g r", g=GROUPS).unsqueeze(2).to_broadcast([P, GROUPS, 4, QD]))
            dve.tensor_copy(wvT[:, 0:D], m_ps[:, 2 * D:3 * D])
            read_m(dve.tensor_copy(wT[:, D:], m_ps[:, 3 * D:]))
            misc("ctx", 0)
            dve.wait_ge(m_full, M["b1", 0])
            read_m(dve.tensor_copy(w1_sb[:, :, F:], m_ps[:, 0:E * KF].rearrange("p (e k) -> p e k", k=KF)))
            misc("norm1", 0)
            stats1(1)
            misc("q", 0)
            dve.wait_ge(ld_c, 32)
            misc("k", 0)
            dve.wait_ge(set_p, 3)
            for b in range(B):
                last = dve.tensor_copy(vblk[:, b, :, 0:CHEADS * VW].rearrange("p c (h w) -> p c h w", w=VW)[:, :, :, HD],
                                       C("vmask").rearrange("p (c h) -> p c h", c=CH))
            do(last)
            misc("v", 0)
            misc("norm1", 1)
            dve.tensor_copy(upper_b[:], C("upper"))
            do(dve.tensor_copy(ones_b[:], C("ones")))
            for b in range(2, B):
                stats1(b)
            softmax(0)
            def slot_of(n, k):
                for step in slot_steps(n, k):
                    misc(*step)

            for n in range(TILES):
                slot_of(n, 0)
                if n + 1 < TILES:
                    softmax(n + 1)
                slot_of(n, 1)
                normalise(n)
                slot_of(n, 2)
            for name in POST:
                misc(name, B - 1)
            dve.tensor_copy(carryb[:], carry[:]).then_inc(cast_done, 1)
            dve.wait_ge(m_full, M["count", 0])
            cnt = m_ps[:, 0:E]
            dve.tensor_tensor(tbi[:, 2, :], cnt, C("ebase"), ALU.add).then_inc(counts_done, 1)
            do(dve.tensor_scalar(tbi[:, 0, :], cnt, float(P - 1), None, ALU.add))
            do(dve.tensor_single_scalar(tbi[:, 1, :], tbi[:, 0, :], 7, ALU.logical_shift_right))
            do(dve.tensor_copy(tb[:, 0, :], tbi[:, 1, :]))
            do(dve.tensor_tensor(cmp[:, 0, 0:E * E].rearrange("p (a b) -> p a b", a=E), C("le").rearrange("p (a b) -> p a b", a=E),
                                 tb[:, 0, :].unsqueeze(1).to_broadcast([P, E, E]), ALU.mult))
            do(dve.tensor_reduce(tb[:, 1, :], cmp[:, 0, 0:E * E].rearrange("p (a b) -> p a b", a=E), AX, ALU.add))
            je = lambda a: a.rearrange("p (j e) -> p j e", e=E)
            jb = lambda a: a.unsqueeze(1).to_broadcast([P, NT, E])
            do(dve.tensor_tensor(je(cmp[:, 1, :]), jb(tb[:, 1, :]), je(C("tile")), ALU.is_le))
            do(dve.tensor_tensor(je(cmp[:, 2, :]), je(cmp[:, 1, :]), jb(tb[:, 0, :]), ALU.mult))
            do(dve.tensor_reduce(tj[:, 0, :], je(cmp[:, 1, :]), AX, ALU.add))
            do(dve.tensor_reduce(tj[:, 1, :], je(cmp[:, 2, :]), AX, ALU.add))
            do(dve.scalar_tensor_tensor(tj[:, 2, :], tj[:, 1, :], -float(P), C("tile128"), ALU.mult, ALU.add))
            do(dve.scalar_tensor_tensor(tj[:, 3, :], tj[:, 0, :], float(REG), tj[:, 2, :], ALU.mult, ALU.add))
            dve.tensor_scalar(first_row[:], tj[:, 3, :], float(PADROW), None, ALU.min)
            dve.tensor_scalar(tile_expert[:], tj[:, 0, :], float(E - 1), None, ALU.min).then_inc(tab_done, 1)
            dve.wait_ge(exp_w, 1)
            do(dve.tensor_scalar(wts[:, 1, :], wts[:, 0, :], 1.0, None, ALU.add))
            do(dve.reciprocal(wts[:, 1, :], wts[:, 1, :]))
            do(dve.tensor_scalar(wts[:, 2, :], wts[:, 1, :], tg[:, 1:2], None, ALU.mult))
            dve.tensor_tensor(wts[:, 3, :], wts[:, 0, :], wts[:, 2, :], ALU.mult).then_inc(wts_done, 1)
            dve.wait_ge(tab_done, 1)
            dve.wait_ge(ld_e, 16 * (2 + KF))

            def weights(i, c, ex):
                j, u, r, w = tile(i, c)
                if c >= U:
                    dve.wait_ge(h_done, j - U + 1)
                dve.tensor_copy(w1_now[:, u:u + 1, :], w1_sb[:, ds(ex, 1), :]).then_inc(w1_ready, 1)

            def result(i, c, ex):
                j, u, r, w = tile(i, c)
                dve.wait_ge(dn_full, j + 1)
                if c >= R:
                    dve.wait_ge(y_out[r], 16 * w)
                dve.tensor_tensor(yt[:, r, :].unsqueeze(1), y_ps.unsqueeze(1), b2_bc[:, ds(ex, 1), :], ALU.add).then_inc(y_done, 1)

            def step(i, c, ex, ahead):
                weights(i, c + 2, ahead)
                result(i, c, ex)

            ex = load_experts(DVE, 0, 0, R + 2)
            weights(0, 0, ex[0])
            weights(0, 1, ex[1])
            for c in range(R):
                step(0, c, ex[c], ex[c + 2])
            with dve.Fori(0, NT // R - 1) as i:
                ex = load_experts(DVE, i, R, R + 2)
                for c in range(R, 2 * R):
                    step(i, c, ex[c - R], ex[c - R + 2])
            i = NT // R - 1
            ex = load_experts(DVE, i, R, NT % R)
            for c in range(NT % R - 2):
                step(i, R + c, ex[c], ex[c + 2])
            for c in range(NT % R - 2, NT % R):
                result(i, R + c, ex[c])
            for b in range(B):
                dve.wait_ge(ld_y[b], 16)
                for t in range(T):
                    n = T * b + t
                    last = dve.scalar_tensor_tensor(acc[:, n, :], yy[:, b, t, 0:D], wts[:, 2, n:n + 1], x1[:, n, :], ALU.mult, ALU.add)
                do(last)
                for t in range(T):
                    n = T * b + t
                    last = dve.scalar_tensor_tensor(res[:, n, :], yy[:, b, t, D:2 * D], wts[:, 3, n:n + 1], acc[:, n, :], ALU.mult, ALU.add)
                last.then_inc(res_done, 1)

        @block.gpsimd
        def _(pool):
            pool.memset(wvT[:, D:], 0.0).then_inc(set_p, 1)
            pool.memset(wg_sb[:, E:], 0.0).then_inc(set_p, 1)
            pool.memset(vblk[:], 0.0).then_inc(set_p, 1)
            steps = [0]

            def done(ins):
                steps[0] += 1
                ins.then_inc(p_step, 1)
                pool.wait_ge(p_step, steps[0])

            def k_block(b):
                pool.wait_ge(m_read, M["k", b])
                pool.tensor_tensor(kblk[:, b, :].rearrange("p (g h k) -> p g h k", g=GROUPS, k=KEYS),
                                   k_rows[:].bitcast(f32).rearrange("p (g k) -> p g k", g=GROUPS).unsqueeze(2).to_broadcast([P, GROUPS, GRP, KEYS]),
                                   C("kmask").unsqueeze(1).unsqueeze(3).to_broadcast([P, GROUPS, GRP, KEYS]), ALU.mult).then_inc(k_done, 1)

            def newton_root(b, seeded, half, rs, rooted):
                pool.wait_ge(seeded, b + 1)
                h, y = half[:, T * b:T * b + T], rs[:, T * b:T * b + T]
                for k in range(3):
                    done(pool.tensor_tensor(newton[:], y, y, ALU.mult))
                    done(pool.tensor_tensor(newton[:], newton[:], h, ALU.mult))
                    done(pool.tensor_scalar(newton[:], newton[:], 1.5, None, ALU.add))
                    last = pool.tensor_tensor(y, y, newton[:], ALU.mult)
                    if k < 2:
                        done(last)
                last.then_inc(rooted, 1)
                pool.wait_ge(rooted, b + 1)

            def with_bias(b):
                pool.wait_ge(ld_x[b], 16)
                pool.tensor_tensor(xb[:, T * b:T * b + T, :], x_sb[:, T * b:T * b + T, :],
                                   tbo[:].unsqueeze(1).to_broadcast([P, T, D]), ALU.add).then_inc(xb_done, 1)

            def send(b):
                pool.wait_ge(xs_done, b + 1)
                if b:
                    pool.wait_ge(scat, 16 * 2 * T * b)
                for k in range(2):
                    pool.tensor_copy(rows[:, k, :, 0:D], xs[:])
                    last = pool.tensor_copy(rows[:, k, :, D:ROWW].bitcast(i32),
                                            cint[:, 2 * T * b:2 * T * b + 2 * T].rearrange("p (t k) -> p t k", k=2)[:, :, k:k + 1])
                last.then_inc(rows_done, 1)
                pool.wait_ge(rows_done, b + 1)
                pool.wait_ge(slots_done, b + 1)
                for k in range(2):
                    for t in range(T):
                        pool.indirect_dma_start(out=rows_dram, out_offset=bass.IndirectOffsetOnAxis(ap=slot[:, k * T + t:k * T + t + 1], axis=0),
                                                in_=rows[:, k, t, :], in_offset=None, bounds_check=PADROW + P - 1, oob_is_err=False).then_inc(scat, 16)

            newton_root(0, seed1, half1, rs1, root1)
            newton_root(1, seed1, half1, rs1, root1)
            pool.wait_ge(ld_c, 32)
            k_block(0)
            pool.wait_ge(tanh_done, 1)
            done(pool.tensor_scalar(tbo[:], bo[:], tg[:, 0:1], None, ALU.mult))
            pool.wait_ge(m_read, M["w", 0])
            pool.tensor_scalar(wT[:, D:], wT[:, D:], tg[:, 0:1], None, ALU.mult).then_inc(wout_done, 1)
            for b in range(2, B):
                newton_root(b, seed1, half1, rs1, root1)
            for b in range(B):
                with_bias(b)
                if b + 1 < B:
                    k_block(b + 1)
                if b:
                    newton_root(b - 1, seed2, half2, rs2, root2)
                    send(b - 1)
            newton_root(B - 1, seed2, half2, rs2, root2)
            send(B - 1)
            pool.wait_ge(tab_done, 1)

            def ids(i, c):
                j, u, r, w = tile(i, c)
                pool.wait_ge(x_tile[r], 16 * (w + 1))
                if c >= R:
                    pool.wait_ge(y_out[r], 16 * w)
                at = xg[:, r, D:ROWW].bitcast(i32)
                pool.tensor_tensor(dest[:, r:r + 1], at, cint[:, 2 * TILES:2 * TILES + 1], ALU.add).then_inc(id_done, 1)

            def y_send(i, c):
                j, u, r, w = tile(i, c)
                n = j + 1 if isinstance(i, int) else pool.snap(j + 1)
                pool.wait_ge(id_done, n)
                pool.wait_ge(y_done, n)
                pool.reg_add(bound, last, 1)
                pool.indirect_dma_start(out=y_dram, out_offset=bass.IndirectOffsetOnAxis(ap=dest[:, r:r + 1], axis=0),
                                        in_=yt[:, r, :], in_offset=None, bounds_check=bound, oob_is_err=False).then_inc(y_out[r], 16)

            last, bound = pool.alloc_register("last_result"), pool.alloc_register("bound")
            pool.reg_mov(last, 2 * TOK - 2)
            ids(0, 0)
            for c in range(R - 1):
                ids(0, c + 1)
                y_send(0, c)
            with pool.Fori(0, NT // R - 1) as i:
                for c in range(R - 1, 2 * R - 1):
                    ids(i, c + 1)
                    y_send(i, c)
            i = NT // R - 1
            for c in range(R - 1, NT - R * i - 1):
                ids(i, c + 1)
                y_send(i, c)
            y_send(i, NT - R * i - 1)


_INS = ["x", "ctx_1024", "g_xattn", "g_ffn", "L0_xattn_Wq", "L0_xattn_Wkv", "L0_xattn_Wout", "L0_xattn_bout",
        "L0_ffn_Wg", "L0_ffn_W1", "L0_ffn_b1", "L0_ffn_W2", "L0_ffn_b2"]
_OUTS = [((B, S, D), "float32")]


def kernel(**inputs):
    import numpy as _np
    import concourse.bacc as _bacc
    from concourse import mybir as _mybir
    from concourse.bass_utils import run_bass_kernel_spmd as _run

    nc = _bacc.Bacc("TRN2", target_bir_lowering=False, num_devices=1)
    arrays, args = {}, []
    given = [(n, _np.ascontiguousarray(inputs[n])) for n in _INS]
    for name, a in given + list(zip(("constants", "integers"), constants())):
        arrays[f"in_{name}_dram"] = a
        args.append(nc.dram_tensor(f"in_{name}_dram", a.shape, _mybir.dt.from_np(a.dtype), kind="ExternalInput").ap())
    for i, (shape, dtype) in enumerate(_OUTS):
        dt = _mybir.dt.from_np(_np.dtype(dtype))
        args.append(nc.dram_tensor(f"out_{i}_dram", shape, dt, kind="ExternalOutput").ap())
    flamingo(nc, *args)
    r = _run(nc, [arrays], core_ids=[0])
    return r.results[0]["out_0_dram"]
```

```python
from contextlib import ExitStack

import numpy as np

import concourse.bass as bass
from concourse import mybir

P = 128
B, S, D = 4, 512, 128
KEYS, HEADS, HD = 77, 16, 8
T = S // P
TILES = B * T
GRP = 4
GROUPS = HEADS // GRP
QD = GRP * HD
UNITS = HEADS // (2 * GRP)
HK = HEADS * KEYS
CH = -(-HK // P)
CROWS = [min(P, HK - P * c) for c in range(CH)]
H0 = [P * c // KEYS for c in range(CH)]
CHEADS = 3
VW = HD + 1
NMIN = 64
PTG = [range(0, 4), range(4, 8), range(8, CH)]

E, F, KF = 8, 512, 4
TOK = B * S
REG = TOK + P
PADROW = E * REG
ROWW = D + 1
NOWHERE = 1 << 20
NT = (2 * TOK + E * (P - 1)) // P
PARCELS = [(T * b, T) for b in range(B - 1)] + [(TILES - T, T // 2), (TILES - T // 2, T // 2)]
R = 6
U = 3

_names = [("ident", P), ("upper", P), ("ones", P), ("kmask", GRP), ("klow", 1), ("qlow", 1), ("vmask", CH * CHEADS), ("ebase", E),
          ("expert", E), ("le", E * E), ("tile", NT * E), ("tile128", NT)]
CC, _o = {}, 0
for _n, _w in _names:
    CC[_n] = (_o, _o + _w)
    _o += _w
CW = _o


def constants():
    c = np.zeros((P, CW), np.float32)
    put = lambda n, a: c.__setitem__((slice(None), slice(*CC[n])), np.asarray(a, np.float32).reshape(-1, CC[n][1] - CC[n][0]))
    p = np.arange(P)
    put("ident", np.eye(P))
    put("upper", p[:, None] < p[None, :])
    put("ones", np.ones((P, P)))
    put("kmask", p[:, None] % QD // HD == np.arange(GRP))
    put("qlow", np.where(p[:, None] // QD % 2, -1, 0))
    put("klow", np.where(p[:, None] >= P // 2, -1, 0))
    head = (P * np.arange(CH)[None, :, None] + p[:, None, None]) // KEYS
    want = np.array(H0)[None, :, None] + np.arange(CHEADS)
    put("vmask", (head == want) & (head < HEADS))
    put("ebase", np.tile(REG * np.arange(E), (P, 1)))
    put("expert", np.tile(np.arange(E), (P, 1)))
    put("le", np.tile((np.arange(E)[None, :] <= np.arange(E)[:, None]).reshape(-1), (P, 1)))
    put("tile", np.tile(np.repeat(np.arange(NT), E), (P, 1)))
    put("tile128", np.tile(P * np.arange(NT), (P, 1)))
    ids = 2 * (P * np.arange(TILES)[None, :, None] + p[:, None, None]) + np.arange(2)
    i = np.concatenate([ids.reshape(P, -1), np.zeros((P, D)), np.full((P, 1), NOWHERE)], 1)
    return c, i.astype(np.int32)


def flamingo(nc, x, ctx, g_x, g_f, wq, wkv, wout, bout, wg, w1, b1, w2, b2, cf, ci, out):
    f32, f32r, bf16, i32 = mybir.dt.float32, mybir.dt.float32r, mybir.dt.bfloat16, mybir.dt.int32
    ALU, ACT, AX = mybir.AluOpType, mybir.ActivationFunctionType, mybir.AxisListType.X
    ds = bass.ds
    PE, DVE, SP = mybir.EngineType.PE, mybir.EngineType.DVE, mybir.EngineType.SP
    st = ExitStack()
    with st:
        sb = lambda n, s, d=f32: st.enter_context(nc.sbuf_tensor(n, s, d))
        pb = lambda n, s, d=f32: st.enter_context(nc.psum_tensor(n, s, d))
        sem = lambda n: st.enter_context(nc.semaphore(n))

        rows_dram = nc.dram_tensor("rows_by_expert", [PADROW + P, ROWW], f32, kind="Internal").ap()
        q_dram = nc.dram_tensor("q_parts_dram", [B, 2, P, S], f32, kind="Internal").ap()
        y_dram = nc.dram_tensor("expert_results", [2 * TOK, D], f32, kind="Internal").ap()

        cst = sb("cst", [P, CW])
        cint = sb("cint", [P, 2 * TILES + ROWW], i32)
        C = lambda n: cst[:, CC[n][0]:CC[n][1]]
        ident = C("ident")
        w_in = sb("w_in", [P, 4, D])
        wT = sb("wT", [P, 2 * D])
        wvT = sb("wvT", [P, D + NMIN])
        wg_sb = sb("wg_sb", [P, NMIN])
        gates = sb("gates", [P, 2])
        tg = sb("tg", [P, 2])
        bo = sb("bo", [P, D])
        tbo = sb("tbo", [P, D])
        w1_sb = sb("w1_sb", [P, E, F + KF])
        w1_now = sb("w1_now", [P, U, F + KF])
        b1_in = sb("b1_in", [E * KF, P])
        w2_sb = sb("w2_sb", [P, E, KF, D])
        b2_bc = sb("b2_bc", [P, E, D])
        x_sb = sb("x_sb", [P, TILES, D])
        xb = sb("xb", [P, TILES, D])
        x1 = sb("x1", [P, TILES, D])
        ctx_sb = sb("ctx_sb", [KEYS, B, D])
        ctxT = sb("ctxT", [P, B, 3, KEYS])
        wk_rep = sb("wk_rep", [P, GROUPS, 4, QD])
        wq_rep = sb("wq_rep", [P, GROUPS, 4, QD])
        k_high = sb("k_high", [P, GROUPS * KEYS], f32r)
        k_rows = sb("k_rows", [P, GROUPS * KEYS], f32r)
        kblk = sb("kblk", [P, B, HK], f32r)
        q_parts = sb("q_parts", [P, 2, S], f32r)
        q_rows = sb("q_rows", [P, 2, GROUPS, S], f32r)
        vblk = sb("vblk", [P, B, CH, NMIN])
        stat1, mv1, rs1 = sb("stat1", [P, T, 6]), sb("mv1", [P, TILES, 2]), sb("rs1", [P, TILES])
        stat2, mv2, rs2 = sb("stat2", [P, T, 6]), sb("mv2", [P, TILES, 2]), sb("rs2", [P, TILES])
        half1, half2 = sb("half1", [P, TILES]), sb("half2", [P, TILES])
        guess = sb("guess", [P, 2, T])
        newton = sb("newton", [P, T])
        xn = sb("xn", [P, T, D])
        xnT = sb("xnT", [P, S])
        smax = sb("smax", [P, 2, HEADS])
        dif = sb("dif", [P, 2, HK])
        prob = sb("prob", [P, 2, HK])
        pT = sb("pT", [P, 2, CH * P])
        rsum = sb("rsum", [P, HEADS])
        attn = sb("attn", [P, T, D])
        attnT = sb("attnT", [P, S])
        xs = sb("xs", [P, T, D])
        xsT = sb("xsT", [P, S])
        lg = sb("lg", [P, T, E])
        top = sb("top", [P, T, 8])
        topi = sb("topi", [P, T, 8], mybir.dt.uint32)
        topf = sb("topf", [P, 2, T])
        oh = sb("oh", [P, 2, T, E])
        ohb = sb("ohb", [P, T, E], bf16)
        ohsum = sb("ohsum", [P, T, E])
        carry = sb("carry", [P, E])
        carryb = sb("carryb", [P, E], bf16)
        csum = sb("csum", [P, E])
        upper_b, ones_b = sb("upper_b", [P, P], bf16), sb("ones_b", [P, P], bf16)
        pos = sb("pos", [P, T, E])
        posk = sb("posk", [P, 2, T, E])
        slotf = sb("slotf", [P, 2, T])
        slot = sb("slot", [P, 2, T], i32)
        slot_last = sb("slot_last", [P, 2, T], i32)
        rows = sb("rows", [P, 2, T, ROWW])
        rows_last = sb("rows_last", [P, 2, T, ROWW])
        gap = sb("gap", [P, TILES])
        wts = sb("wts", [P, 4, TILES])
        tb = sb("tb", [P, 4, E])
        tbi = sb("tbi", [P, 3, E], i32)
        cmp = sb("cmp", [P, 3, NT * E])
        tj = sb("tj", [P, 4, NT])
        first_row = sb("first_row", [P, NT], i32)
        tile_expert = sb("tile_expert", [P, NT], i32)
        xg = sb("xg", [P, R, ROWW])
        xgT = sb("xgT", [P, U, P])
        hT = dif[:].rearrange("p a n -> p (a n)")[:, 0:U * F].rearrange("p (u f) -> p u f", u=U)
        yt = sb("yt", [P, R, D])
        dest = sb("dest", [P, R], i32)
        yy = kblk[:].bitcast(f32).rearrange("p b n -> p (b n)")[:, 0:TILES * 2 * D].rearrange("p (b t d) -> p b t d", b=B, t=T)
        acc, res = xb, x_sb
        second = prob[:].rearrange("p a n -> p (a n)")[:, 0:TILES * D].rearrange("p (n d) -> p n d", n=TILES)

        sc_ps = pb("sc_ps", [P, 4, 512])
        pt_ps = pb("pt_ps", [P, 2, 512])
        o_ps = pb("o_ps", [P, 512])
        m_ps = pb("m_ps", [P, 512])
        up_ps = sc_ps[:, 0:U, :]
        xt_ps, y_ps = pt_ps[:, 0, 0:P], pt_ps[:, 1, 0:D]

        ld_id, ld_c, ld_w, ld_g, ld_wg, ld_e = (sem(n) for n in ("ld_id", "ld_c", "ld_w", "ld_g", "ld_wg", "ld_e"))
        ld_b1 = sem("ld_b1")
        w1_ready = sem("w1_ready")
        wout_done = sem("wout_done")
        counts_done = sem("counts_done")
        ld_x = [sem(f"ld_x{b}") for b in range(B)]
        ld_ctx = sem("ld_ctx")
        f_full = sem("f_full")
        f_copy = sem("f_copy")
        wq_done = sem("wq_done")
        f_rows = sem("f_rows")
        q_high = sem("q_high")
        k_hi = sem("k_hi")
        q_out = sem("q_out")
        q_in = [sem("q_in0"), sem("q_in1")]
        root1, root2 = sem("root1"), sem("root2")
        seed1, seed2 = sem("seed1"), sem("seed2")
        set_p = sem("set_p")
        tanh_done = sem("tanh_done")
        d = sem("d")
        xn_done = sem("xn_done")
        xs_done = sem("xs_done")
        id_done = sem("id_done")
        m_full = sem("m_full")
        m_read = sem("m_read")
        k_done = sem("k_done")
        xb_done = sem("xb_done")
        sc_full = sem("sc_full")
        sc_read = sem("sc_read")
        pr_done = sem("pr_done")
        pt_full = sem("pt_full")
        pt_read = sem("pt_read")
        pv_done = sem("pv_done")
        o_read = sem("o_read")
        cast_done = sem("cast_done")
        slots_done = sem("slots_done")
        rows_done = sem("rows_done")
        p_step = sem("p_step")
        ids_last = sem("ids_last")
        rows_last_done = sem("rows_last_done")
        scat = [sem("scat0"), sem("scat1")]
        tab_done = sem("tab_done")
        padded = sem("padded")
        x_tile = [sem(f"x_tile{r}") for r in range(R)]
        y_out = [sem(f"y_out{r}") for r in range(R)]
        xt_full, xt_read = sem("xt_full"), sem("xt_read")
        up_full, h_done = sem("up_full"), sem("h_done")
        dn_full, y_done = sem("dn_full"), sem("y_done")
        exp_w = sem("exp_w")
        wts_done = sem("wts_done")
        ld_y = [sem(f"ld_y{b}") for b in range(B)]
        second_done = sem("second_done")
        res_done = sem("res_done")
        stored = sem("stored")
        block = st.enter_context(nc.Block())

        def load_table(engine, entries, most):
            _, v = nc.values_load_multi_w_load_instructions(
                entries, engines=[engine], min_val=0, max_val=most,
                skip_runtime_bounds_check_because="the table is made of clipped values")
            return v

        def load_experts(engine, i, c, n):
            return load_table(engine, tile_expert[0:1, ds(i * R + c, n)], E - 1)

        def tile(i, c):
            return i * R + c, c % U, c % R, i + c // R

        def freed(g):
            return g - 1 if g < B else B - 2

        def at_parcel(g):
            n, k = PARCELS[g]
            return slice(n % T, n % T + k), slice(n, n + k)

        def sent(g):
            return scat[g % 2], 16 * 2 * sum(PARCELS[h][1] for h in range(g % 2, g + 1, 2))

        AHEAD = {(0, 1): [("xn", 1), ("stats1", 2)], (0, 2): [("q", 1)], (1, 1): [("k", 1)], (2, 1): [("v", 1)], (3, 2): [("norm1", 2)]}
        BEHIND = {(0, 0): [("attn", -1)], (0, 1): [("route", -2)], (1, 0): [("rank", -2)], (1, 2): [("out", -1), ("stats2", -1)],
                  (2, 2): [("norm2", -1)], (3, 1): [("xs", -1)], (3, 2): [("logit", -1)]}
        g = B - 1
        LAST = {(0, 0): [("attn", g - 1)], (0, 1): [("route", g - 2)], (0, 2): [("out", g - 1)], (1, 0): [("rank", g - 2)],
                (1, 1): [("stats2", g - 1)], (2, 1): [("attn", g)], (2, 2): [("out", g), ("norm2", g - 1), ("stats2", g)],
                (3, 0): [("roots", g), ("norm2", g)], (3, 1): [("xs", g - 1)], (3, 2): [("logit", g - 1)]}
        FINISH = [("attn", g + 1), ("route", g - 1), ("out", g + 1), ("rank", g - 1), ("stats2", g + 1), ("roots", g + 1),
                  ("norm2", g + 1), ("xs", g), ("logit", g), ("route", g), ("xs", g + 1), ("rank", g), ("logit", g + 1),
                  ("route", g + 1), ("rank", g + 1)]

        DVE_ONLY = ("stats1", "norm1", "stats2", "norm2", "roots", "route")

        def slot_steps(n, k):
            b, t = divmod(n, T)
            if b == B - 1:
                return LAST.get((t, k), [])
            return [(s, b + at) for s, at in BEHIND.get((t, k), []) + AHEAD.get((t, k), []) if 0 <= b + at < B]

        order = [("w", 0), ("k", 0), ("b1", 0), ("v", 0)]
        for n in range(TILES):
            for k in range(3):
                order += slot_steps(n, k)
        order += FINISH
        M = {s: i + 1 for i, s in enumerate(s for s in order + [("count", 0)] if s[0] not in DVE_ONLY)}

        def tail(queue, e):
            row = queue.value_load(tbi[0:1, 2, e:e + 1], min_val=REG * e, max_val=REG * e + TOK)
            queue.dma_start(rows_dram[ds(row, P), :], cint[:, 2 * TILES:].bitcast(f32)).then_inc(padded, 16)

        @block.sync
        def _(sp):
            sp.dma_start(x_sb[:, 0:T, :], x[0].rearrange("(t p) d -> p t d", p=P)).then_inc(ld_x[0], 16)
            sp.dma_start(ident, cf[:, 0:P]).then_inc(ld_id, 16)
            sp.dma_start(cst[:, P:], cf[:, P:]).then_inc(ld_c, 16)
            sp.dma_start(ctx_sb[:], ctx.rearrange("b k d -> k b d")).then_inc(ld_ctx, 16)
            sp.dma_start(wg_sb[:, 0:E], wg).then_inc(ld_wg, 16)
            sp.dma_start(b1_in[:], b1.rearrange("e (k p) -> (e k) p", k=KF)).then_inc(ld_b1, 16)
            for b in range(1, B):
                sp.dma_start(x_sb[:, T * b:T * b + T, :], x[b].rearrange("(t p) d -> p t d", p=P)).then_inc(ld_x[b], 16)

            def spread_q(b):
                sp.wait_ge(m_read, M["q", b])
                sp.dma_start(q_dram[b].rearrange("h p s -> p h s"), q_parts[:].bitcast(f32)).then_inc(q_out, 16)
                sp.wait_ge(q_out, 16 * b)
                if b >= 2:
                    sp.wait_ge(sc_full, UNITS * T * (b - 1))
                for k in range(4):
                    sp.dma_start(q_rows[QD * k:QD * k + QD, b % 2, :, :].bitcast(f32),
                                 q_dram[b, k % 2].rearrange("(g r) s -> r g s", r=QD)).then_inc(q_in[b % 2], 16)

            sp.dma_start(w1_sb[:, :, 0:F], w1.rearrange("e d f -> d e f")).then_inc(ld_e, 16)
            for k in range(KF):
                sp.dma_start(w2_sb[:, :, k, :], w2[:, k * P:k * P + P, :].rearrange("e f d -> f e d")).then_inc(ld_e, 16)
            sp.dma_start(b2_bc[:].rearrange("p e d -> p (e d)"), b2.rearrange("e f -> (e f)").rearrange("(o n) -> o n", o=1).to_broadcast([P, E * D])).then_inc(ld_e, 16)
            for b in range(1, B):
                spread_q(b)
            pad = cint[:, 2 * TILES:].bitcast(f32)
            sp.wait_ge(ld_c, 32)
            sp.dma_start(rows_dram[PADROW:PADROW + P, :], pad).then_inc(padded, 16)
            sp.wait_ge(counts_done, 1)
            for e in range(0, E, 2):
                tail(sp, e)
            sp.wait_ge(tab_done, 1)
            first = load_table(SP, first_row[0:1, 0:R], PADROW)
            sp.wait_ge(padded, 16 * (E + 1))
            for g in (len(PARCELS) - 2, len(PARCELS) - 1):
                sp.wait_ge(*sent(g))

            def load(i, c, row):
                j, _, r, _ = tile(i, c)
                if c >= R:
                    sp.wait_ge(xt_full, j - R + 1)
                    sp.wait_ge(id_done, j - R + 1)
                sp.dma_start(xg[:, r, :], rows_dram[ds(row, P), :]).then_inc(x_tile[r], 16)

            for c in range(R):
                load(0, c, first[c])
            with sp.Fori(0, NT // R - 1) as i:
                row = load_table(SP, first_row[0:1, ds(i * R + R, R)], PADROW)
                for c in range(R):
                    load(i, R + c, row[c])
            row = load_table(SP, first_row[0:1, NT - NT % R:], PADROW)
            for c in range(NT % R):
                load(NT // R - 1, R + c, row[c])
            for r in range(R):
                sp.wait_ge(y_out[r], 16 * len(range(r, NT, R)))
            for b in range(B):
                sp.dma_start(yy[:, b, :, :], y_dram[2 * S * b:2 * S * (b + 1), :]
                             .rearrange("(t p k) d -> p t (k d)", p=P, k=2)).then_inc(ld_y[b], 16)
            for b in range(B):
                sp.wait_ge(res_done, b + 1)
                sp.dma_start(out[b].rearrange("(t p) d -> p t d", p=P), res[:, T * b:T * b + T, :]).then_inc(stored, 16)
            sp.wait_ge(stored, 16 * B)

        @block.tensor
        def _(pe):
            def use(step):
                if M[step] > 1:
                    pe.wait_ge(m_read, M[step] - 1)

            def misc(name, b):
                if name in DVE_ONLY:
                    return
                if name == "rank":
                    pe.wait_ge(cast_done, b + 1)
                    use((name, b))
                    lo, n = PARCELS[b][0] % T, PARCELS[b][1]
                    rk = m_ps[:, 0:n * E]
                    pe.matmul(rk, upper_b[:], ohb[:, lo:lo + n, :].rearrange("p t e -> p (t e)"), start=True, stop=False, skip_group_check=True)
                    for k in range(1, n):
                        pe.matmul(rk[:, k * E:], ones_b[:], ohb[:, lo:lo + n - k, :].rearrange("p t e -> p (t e)"),
                                  start=False, stop=False, skip_group_check=True)
                    for k in range(n):
                        mm = pe.matmul(rk[:, k * E:k * E + E], ones_b[:], carryb[:], start=False, stop=k == n - 1, skip_group_check=True)
                    mm.then_inc(m_full, 1)
                    return
                use((name, b))
                if name == "b1":
                    pe.wait_ge(ld_b1, 16)
                    mm = pe.transpose(m_ps[:, 0:E * KF], b1_in[:], ident[0:E * KF, 0:E * KF])
                elif name == "k":
                    for g in range(GROUPS):
                        mm = pe.matmul(m_ps[:, g * KEYS:g * KEYS + KEYS], wk_rep[:, g, :, :].rearrange("p a b -> p (a b)"),
                                       ctxT[:, b, 0, :], start=True, stop=True, skip_group_check=True)
                elif name == "v":
                    if b == 0:
                        pe.wait_ge(set_p, 3)
                    for c in range(CH):
                        o = P * c % KEYS
                        mm = pe.matmul(m_ps[0:P, c * CHEADS * HD:c * CHEADS * HD + NMIN], ctxT[:, b, :, :].rearrange("p r k -> p (r k)")[:, o:o + P],
                                       wvT[:, H0[c] * HD:H0[c] * HD + NMIN], start=True, stop=True, skip_group_check=True)
                elif name in ("xn", "attn", "xs"):
                    if name == "attn":
                        pe.wait_ge(o_read, sum(PARCELS[b]))
                    else:
                        pe.wait_ge(xn_done if name == "xn" else xs_done, b + 1)
                    src = {"xn": xn, "attn": attn, "xs": xs if b < B - 1 else rows_last[:, 0, :, 0:D]}[name]
                    ts = slice(0, T) if name == "xn" else at_parcel(b)[0]
                    for t in range(ts.start, ts.stop):
                        mm = pe.transpose(m_ps[:, t * P:t * P + P], src[:, t, :], ident)
                elif name == "q":
                    mm = pe.matmul(m_ps[:], wT[:, 0:D], xnT[:], start=True, stop=True)
                elif name == "out":
                    if b == 0:
                        pe.wait_ge(wout_done, 1)
                    ts = at_parcel(b)[0]
                    for t in range(ts.start, ts.stop):
                        mm = pe.matmul(m_ps[:, t * P:t * P + P], attnT[:, t * P:t * P + P], wT[:, D:], start=True, stop=True, skip_group_check=True)
                elif name == "logit":
                    if b == 0:
                        pe.wait_ge(ld_wg, 16)
                    ts = at_parcel(b)[0]
                    for t in range(ts.start, ts.stop):
                        mm = pe.matmul(m_ps[:, t * NMIN:t * NMIN + NMIN], xsT[:, t * P:t * P + P], wg_sb[:], start=True, stop=True, skip_group_check=True)
                mm.then_inc(m_full, 1)

            def scores(n):
                b, t = divmod(n, T)
                if t == 0 and b:
                    pe.wait_ge(q_in[b % 2], 16 * 4 * ((b + 1) // 2))
                if t == 0:
                    pe.wait_ge(k_done, b + 1)
                for u in range(UNITS):
                    i = n * UNITS + u
                    if i >= 2:
                        pe.wait_ge(sc_read, i - 1)
                    if n == 0:
                        pe.wait_ge(f_rows, 2 * u + 2)
                    for g in range(2):
                        h = (2 * u + g) * GRP * KEYS
                        mm = pe.matmul(sc_ps[:, 2 * (i % 2) + g, 0:GRP * KEYS], q_rows[:, b % 2, 2 * u + g, t * P:t * P + P],
                                       kblk[:, b, h:h + GRP * KEYS], start=True, stop=True)
                    mm.then_inc(sc_full, 1)

            def turn_probs(n, groups):
                pe.wait_ge(pr_done, n + 1)
                for g in groups:
                    cs = PTG[g]
                    i = n * len(PTG) + g
                    if i >= 2:
                        pe.wait_ge(pt_read, i - 1)
                    for k, c in enumerate(cs):
                        mm = pe.transpose(pt_ps[0:CROWS[c], i % 2, k * P:k * P + P], prob[:, n % 2, c * P:c * P + CROWS[c]], ident)
                    mm.then_inc(pt_full, 1)

            def values(n):
                b, t = divmod(n, T)
                if n >= 1:
                    pe.wait_ge(o_read, n)
                if t == 0:
                    pe.wait_ge(m_read, M["v", b])
                for g, cs in enumerate(PTG):
                    pe.wait_ge(pt_read, n * len(PTG) + g + 1)
                    for c in cs:
                        mm = pe.matmul(o_ps[:, H0[c] * VW:H0[c] * VW + NMIN], pT[0:CROWS[c], n % 2, c * P:c * P + P],
                                       vblk[0:CROWS[c], b, c, :],
                                       start=c == 0, stop=c == CH - 1, skip_group_check=True)
                mm.then_inc(pv_done, 1)

            pe.wait_ge(ld_id, 16)
            pe.wait_ge(ld_w, 48)
            for k in range(4):
                mm = pe.transpose(m_ps[:, k * D:k * D + D], w_in[:, k, :], ident)
            mm.then_inc(m_full, 1)
            pe.wait_ge(ld_ctx, 16)
            for k in range(B):
                mm = pe.transpose(pt_ps[:, 0, k * KEYS:k * KEYS + KEYS], ctx_sb[:, k, :], ident[0:KEYS, 0:KEYS])
            mm.then_inc(f_full, 1)
            pe.wait_ge(f_copy, 1)
            misc("k", 0)
            pe.wait_ge(xn_done, 1)
            for t in range(T):
                mm = pe.transpose(pt_ps[:, 1, t * P:t * P + P], xn[:, t, :], ident)
            mm.then_inc(f_full, 1)
            pe.wait_ge(f_copy, 2)
            pe.wait_ge(wq_done, 1)
            for g in range(GROUPS):
                pe.matmul(sc_ps[:, g, :], wq_rep[:, g, :, :].rearrange("p a b -> p (a b)"), xnT[:],
                          start=True, stop=True).then_inc(f_full, 1)
            misc("b1", 0)
            scores(0)
            misc("v", 0)

            def slot_of(n, k):
                for step in slot_steps(n, k):
                    misc(*step)

            for n in range(TILES):
                if n + 1 < TILES:
                    scores(n + 1)
                slot_of(n, 0)
                turn_probs(n, (0, 1))
                slot_of(n, 1)
                turn_probs(n, (2,))
                values(n)
                slot_of(n, 2)
            for step in FINISH:
                misc(*step)
            use(("count", 0))
            pe.wait_ge(cast_done, len(PARCELS) + 1)
            pe.matmul(m_ps[:, 0:E], ones_b[:], carryb[:], start=True, stop=True).then_inc(m_full, 1)

            def x_turn(i, c):
                j, u, r, w = tile(i, c)
                pe.wait_ge(x_tile[r], 16 * (w + 1))
                if c:
                    pe.wait_ge(xt_read, j)
                pe.transpose(xt_ps, xg[:, r, 0:D], ident).then_inc(xt_full, 1)

            def up(i, c):
                j, u, r, w = tile(i, c)
                pe.wait_ge(xt_read, j + 1)
                pe.wait_ge(w1_ready, j + 1)
                if c >= U:
                    pe.wait_ge(h_done, j - U + 1)
                for k in range(KF):
                    mm = pe.matmul(up_ps[:, u, k * P:k * P + P], w1_now[:, u, k * P:k * P + P], xgT[:, u, :],
                                   start=True, stop=True, skip_group_check=True)
                mm.then_inc(up_full, 1)

            def down(i, c, ex):
                j, u, r, w = tile(i, c)
                pe.wait_ge(h_done, j + 1)
                if c:
                    pe.wait_ge(y_done, j)
                for k in range(KF):
                    mm = pe.matmul(y_ps, hT[:, u, k * P:k * P + P], w2_sb[:, ds(ex, 1), k, :], start=k == 0, stop=k == KF - 1)
                mm.then_inc(dn_full, 1)

            def step(i, c, ex, turn=True):
                if turn:
                    x_turn(i, c + 1)
                up(i, c)
                down(i, c - 1, ex)

            pe.wait_ge(tab_done, 1)
            pe.wait_ge(ld_e, 16 * (2 + KF))
            x_turn(0, 0)
            x_turn(0, 1)
            up(0, 0)
            ex = load_experts(PE, 0, 0, 1)
            step(0, 1, ex[0])
            with pe.Fori(0, NT // R) as i:
                x_turn(i, 3)
                up(i, 2)
                ex = load_experts(PE, i, 1, R)
                down(i, 1, ex[0])
                for c in range(3, 2 + R):
                    step(i, c, ex[c - 2])
            i = NT // R
            ex = load_experts(PE, i, 1, 2)
            step(i, 2, ex[0], turn=False)
            down(i, 2, ex[1])

        @block.scalar
        def _(act):
            act.dma_start(w_in[:, 0, :], wq).then_inc(ld_w, 16)
            act.dma_start(w_in[:, 1:3, :], wkv.rearrange("(k o) i -> o k i", k=2)).then_inc(ld_w, 16)
            act.dma_start(w_in[:, 3, :], wout).then_inc(ld_w, 16)
            act.dma_start(cint[:], ci).then_inc(ld_c, 16)
            act.dma_start(gates[:, 0:1], g_x.rearrange("(o n) -> o n", o=1).to_broadcast([P, 1])).then_inc(ld_g, 16)
            act.dma_start(gates[:, 1:2], g_f.rearrange("(o n) -> o n", o=1).to_broadcast([P, 1])).then_inc(ld_g, 16)
            act.dma_start(bo[:], bout.rearrange("(o n) -> o n", o=1).to_broadcast([P, D])).then_inc(ld_g, 16)

            def misc(name, b):
                if name not in ("b1", "k", "q", "xn", "attn", "xs", "logit"):
                    return
                act.wait_ge(m_full, M[name, b])
                if name == "k":
                    if b:
                        act.wait_ge(m_read, M["k", b - 1])
                    act.activation(k_high[:], m_ps[:, 0:GROUPS * KEYS], ACT.Copy).then_inc(k_hi, 1)
                elif name == "q":
                    if b == 1:
                        act.wait_ge(f_rows, GROUPS)
                    else:
                        act.wait_ge(q_out, 16 * (b - 1))
                    act.activation(q_parts[:, 0, :], m_ps[:], ACT.Copy).then_inc(q_high, 1)
                elif name == "b1":
                    act.activation(w1_sb[:, :, F:], m_ps[:, 0:E * KF].rearrange("p (e k) -> p e k", k=KF), ACT.Copy).then_inc(m_read, 1)
                elif name == "logit":
                    if b:
                        act.wait_ge(slots_done, freed(b) + 1)
                    ts = at_parcel(b)[0]
                    act.activation(lg[:, ts, :], m_ps[:, 0:T * NMIN].rearrange("p (t n) -> p t n", n=NMIN)[:, ts, 0:E], ACT.Copy).then_inc(m_read, 1)
                else:
                    dst = {"xn": xnT, "attn": attnT, "xs": xsT}[name]
                    ts = slice(0, T) if name == "xn" else at_parcel(b)[0]
                    w = slice(ts.start * P, ts.stop * P)
                    act.activation(dst[:, w], m_ps[:, w], ACT.Copy).then_inc(m_read, 1)

                if name == "xs" and b >= B - 1:
                    act.wait_ge(xs_done, b + 1)
                    act.activation(rows_last[:, 1, ts, 0:D], rows_last[:, 0, ts, 0:D], ACT.Copy).then_inc(rows_last_done, 1)

            def exps(n):
                act.wait_ge(sc_read, UNITS * (n + 1))
                if n >= 2:
                    act.wait_ge(pt_full, len(PTG) * (n - 1))
                act.activation(prob[:, n % 2, :], dif[:, n % 2, :], ACT.Exp).then_inc(pr_done, 1)

            def evac(n):
                if n >= 2:
                    act.wait_ge(pv_done, n - 1)
                for g, cs in enumerate(PTG):
                    i = n * len(PTG) + g
                    act.wait_ge(pt_full, i + 1)
                    full = [c for c in cs if CROWS[c] == P]
                    w = len(full) * P
                    o = cs[0] * P
                    a = act.activation(pT[:, n % 2, o:o + w], pt_ps[:, i % 2, 0:w], ACT.Copy)
                    if len(full) < len(cs):
                        r = CROWS[-1]
                        a = act.activation(pT[0:r, n % 2, o + w:o + w + P], pt_ps[0:r, i % 2, w:w + P], ACT.Copy)
                    a.then_inc(pt_read, 1)

            act.wait_ge(f_full, 1)
            for k in range(3):
                a = act.activation(ctxT[:, :, k, :], pt_ps[:, 0, 0:B * KEYS].rearrange("p (b k) -> p b k", k=KEYS), ACT.Copy)
            a.then_inc(f_copy, 1)
            misc("k", 0)
            act.wait_ge(f_full, 2)
            act.activation(xnT[:], pt_ps[:, 1, :], ACT.Copy).then_inc(f_copy, 1)
            for g in range(GROUPS):
                act.wait_ge(f_full, 3 + g)
                if g >= 2:
                    act.wait_ge(f_rows, g - 1)
                act.activation(q_parts[:, g % 2, :], sc_ps[:, g, :], ACT.Copy).then_inc(f_copy, 1)
            act.wait_ge(ld_g, 48)
            act.activation(tg[:], gates[:], ACT.Tanh).then_inc(tanh_done, 1)
            misc("b1", 0)
            exps(0)

            def slot_of(n, k):
                for step in slot_steps(n, k):
                    misc(*step)

            for n in range(TILES):
                slot_of(n, 0)
                evac(n)
                slot_of(n, 1)
                if n + 1 < TILES:
                    exps(n + 1)
                slot_of(n, 2)
            for step in FINISH:
                misc(*step)
            act.wait_ge(counts_done, 1)
            for e in range(1, E, 2):
                tail(act, e)
            act.activation(wts[:, 0, :], gap[:], ACT.Exp).then_inc(exp_w, 1)

            def x_copy(i, c):
                j, u, r, w = tile(i, c)
                act.wait_ge(xt_full, j + 1)
                if c >= U:
                    act.wait_ge(up_full, j - U + 1)
                act.activation(xgT[:, u, :], xt_ps, ACT.Copy).then_inc(xt_read, 1)

            def relu(i, c):
                j, u, r, w = tile(i, c)
                act.wait_ge(up_full, j + 1)
                if c >= U:
                    act.wait_ge(dn_full, j - U + 1)
                for k in range(KF):
                    a = act.activation(hT[:, u, k * P:k * P + P], up_ps[:, u, k * P:k * P + P], ACT.Relu,
                                       bias=w1_now[:, u, F + k:F + k + 1])
                a.then_inc(h_done, 1)

            def step(i, c):
                x_copy(i, c + 1)
                relu(i, c)

            x_copy(0, 0)
            for c in range(U):
                step(0, c)
            with act.Fori(0, NT // R - 1) as i:
                for c in range(U, U + R):
                    step(i, c)
            i = NT // R - 1
            for c in range(U, NT - R * i - 1):
                step(i, c)
            relu(i, NT - R * i - 1)
            act.wait_ge(wts_done, 1)
            for b in range(B):
                act.wait_ge(ld_y[b], 16)
                for t in range(T):
                    n = T * b + t
                    a = act.activation(second[:, n, :], yy[:, b, t, D:2 * D], ACT.Copy, scale=wts[:, 3, n:n + 1])
                a.then_inc(second_done, 1)

        @block.vector
        def _(dve):
            n_d = [0]

            def do(ins):
                n_d[0] += 1
                ins.then_inc(d, 1)
                dve.wait_ge(d, n_d[0])

            def read_m(ins):
                ins.then_inc(m_read, 1)

            def stats(n, src, stat, mv, half, rs, seeded):
                for t in range(n):
                    last = dve.bn_stats(stat[:, t, :], src[:, t, :])
                do(last)
                for t in range(n):
                    last = dve.bn_aggr(mv[:, t, :], stat[:, t, :])
                do(last)
                v, a = guess[:, 0, 0:n], guess[:, 1, 0:n]
                dve.tensor_scalar(half, mv[:, :, 1], 1e-5, -0.5, ALU.add, ALU.mult)
                do(dve.tensor_scalar(v, mv[:, :, 1], 1e-5, None, ALU.add))
                do(dve.tensor_single_scalar(a.bitcast(i32), v.bitcast(i32), 1, ALU.logical_shift_right))
                dve.tensor_scalar(rs.bitcast(i32), a.bitcast(i32), -1.0, float(0x5F3759DF), ALU.mult, ALU.add).then_inc(seeded, 1)

            def normalised(n, dst, src, mv, rs, signal):
                for t in range(n):
                    last = dve.tensor_scalar(dst[:, t, :], src[:, t, :], mv[:, t, 0:1], rs[:, t:t + 1], ALU.subtract, ALU.mult)
                last.then_inc(signal, 1)

            def bt(a, b):
                return a[:, T * b:T * b + T]

            def stats1(b):
                dve.wait_ge(ld_x[b], 16)
                if b:
                    dve.wait_ge(seed1, b)
                stats(T, bt(x_sb, b), stat1, bt(mv1, b), bt(half1, b), bt(rs1, b), seed1)

            def misc(name, b):
                if name == "stats1":
                    stats1(b)
                elif name == "norm1":
                    dve.wait_ge(root1, b + 1)
                    if b == 1:
                        dve.wait_ge(f_full, 2)
                    elif b:
                        dve.wait_ge(m_full, M["xn", b - 1])
                    normalised(T, xn, bt(x_sb, b), bt(mv1, b), bt(rs1, b), xn_done)
                elif name == "k":
                    dve.wait_ge(k_hi, b + 1)
                    if b:
                        dve.wait_ge(k_done, b)
                    dve.scalar_tensor_tensor(k_rows[:], k_high[:].bitcast(f32), C("klow"), m_ps[:, 0:GROUPS * KEYS],
                                             ALU.mult, ALU.add).then_inc(m_read, 1)
                elif name == "q":
                    dve.wait_ge(q_high, b)
                    dve.tensor_tensor(q_parts[:, 1, :], m_ps[:], q_parts[:, 0, :].bitcast(f32), ALU.subtract).then_inc(m_read, 1)
                elif name == "v":
                    dve.wait_ge(m_full, M[name, b])
                    v = vblk[:, b, :, 0:CHEADS * VW].rearrange("p c (h w) -> p c h w", w=VW)
                    read_m(dve.tensor_tensor(v[:, :, :, 0:HD], m_ps[:, 0:CH * CHEADS * HD].rearrange("p (c h w) -> p c h w", h=CHEADS, w=HD),
                                             C("vmask").rearrange("p (c h) -> p c h", c=CH).unsqueeze(3).to_broadcast([P, CH, CHEADS, HD]), ALU.mult))
                elif name == "out":
                    ts, al = at_parcel(b)
                    w = slice(ts.start * P, ts.stop * P)
                    dve.wait_ge(m_full, M[name, b])
                    dve.wait_ge(xb_done, al.start // T + 1)
                    dve.tensor_tensor(x1[:, al, :].rearrange("p t d -> p (t d)"), m_ps[:, w],
                                      xb[:, al, :].rearrange("p t d -> p (t d)"), ALU.add).then_inc(m_read, 1)
                elif name == "stats2":
                    al = at_parcel(b)[1]
                    dve.wait_ge(m_read, M["out", b])
                    if b:
                        dve.wait_ge(seed2, b)
                    stats(PARCELS[b][1], x1[:, al, :], stat2, mv2[:, al, :], half2[:, al], rs2[:, al], seed2)
                elif name == "roots":
                    al = at_parcel(b)[1]
                    dve.wait_ge(seed2, b + 1)
                    v, y, h = guess[:, 0, 0:PARCELS[b][1]], rs2[:, al], half2[:, al]
                    for _ in range(3):
                        do(dve.tensor_tensor(v, y, y, ALU.mult))
                        do(dve.tensor_tensor(v, v, h, ALU.mult))
                        do(dve.tensor_scalar(v, v, 1.5, None, ALU.add))
                        do(dve.tensor_tensor(y, y, v, ALU.mult))
                elif name == "norm2":
                    ts, al = at_parcel(b)
                    if b < B - 1:
                        dve.wait_ge(root2, b + 1)
                    if 0 < b < B - 1:
                        dve.wait_ge(m_full, M["xs", b - 1])
                        dve.wait_ge(rows_done, b)
                    dst = xs[:, ts, :] if b < B - 1 else rows_last[:, 0, ts, 0:D]
                    normalised(PARCELS[b][1], dst, x1[:, al, :], mv2[:, al, :], rs2[:, al], xs_done)
                elif name == "route":
                    ts, al = at_parcel(b)
                    n = PARCELS[b][1]
                    dve.wait_ge(m_read, M["logit", b])
                    for t in range(ts.start, ts.stop):
                        last = dve.max(top[:, t, :], lg[:, t, :])
                    do(last)
                    for t in range(ts.start, ts.stop):
                        last = dve.max_index(topi[:, t, :], top[:, t, :], lg[:, t, :])
                    do(last)
                    do(dve.tensor_copy(topf[:, :, ts], topi[:, ts, 0:2].rearrange("p t k -> p k t")))
                    dve.tensor_tensor(gap[:, al], top[:, ts, 1], top[:, ts, 0], ALU.subtract)
                    for k in range(2):
                        last = dve.tensor_tensor(oh[:, k, ts, :], C("expert").unsqueeze(1).to_broadcast([P, n, E]),
                                                 topf[:, k, ts].unsqueeze(2).to_broadcast([P, n, E]), ALU.is_equal)
                    do(last)
                    if b:
                        dve.wait_ge(m_full, M["rank", b - 1])
                    dve.tensor_copy(carryb[:], carry[:])
                    do(dve.tensor_tensor(ohsum[:, ts, :], oh[:, 0, ts, :], oh[:, 1, ts, :], ALU.add))
                    dve.tensor_copy(ohb[:, ts, :], ohsum[:, ts, :]).then_inc(cast_done, 1)
                    do(dve.tensor_reduce(csum[:], ohsum[:, ts, :].rearrange("p t e -> p e t"), AX, ALU.add))
                    do(dve.tensor_tensor(carry[:], carry[:], csum[:], ALU.add))
                elif name == "rank":
                    ts, _ = at_parcel(b)
                    n = PARCELS[b][1]
                    dve.wait_ge(m_full, M[name, b])
                    dve.tensor_tensor(pos[:, ts, :], m_ps[:, 0:n * E].rearrange("p (t e) -> p t e", e=E),
                                      C("ebase").unsqueeze(1).to_broadcast([P, n, E]), ALU.add).then_inc(m_read, 1)
                    dve.wait_ge(m_read, M[name, b])
                    for k in range(2):
                        last = dve.tensor_tensor(posk[:, k, ts, :], oh[:, k, ts, :], pos[:, ts, :], ALU.mult)
                    do(last)
                    do(dve.tensor_reduce(slotf[:, :, ts], posk[:, :, ts, :], AX, ALU.add))
                    if 0 < b < B - 1:
                        dve.wait_ge(*sent(b - 1))
                    dve.tensor_copy((slot if b < B - 1 else slot_last)[:, :, ts], slotf[:, :, ts]).then_inc(slots_done, 1)

            def softmax(n):
                for u in range(UNITS):
                    i = n * UNITS + u
                    dve.wait_ge(sc_full, i + 1)
                    s = sc_ps[:, 2 * (i % 2):2 * (i % 2) + 2, 0:GRP * KEYS].rearrange("p g (h k) -> p g h k", k=KEYS)
                    m = smax[:, u, 0:2 * GRP].rearrange("p (g h) -> p g h", g=2)
                    do(dve.tensor_reduce(m, s, AX, ALU.max))
                    if u == 0 and n >= 2:
                        dve.wait_ge(pr_done, n - 1)
                    o = dif[:, n % 2, u * 2 * GRP * KEYS:(u + 1) * 2 * GRP * KEYS].rearrange("p (g h k) -> p g h k", g=2, k=KEYS)
                    dve.tensor_tensor(o, s, m.unsqueeze(3).to_broadcast([P, 2, GRP, KEYS]), ALU.subtract).then_inc(sc_read, 1)

            def normalise(n):
                b, t = divmod(n, T)
                dve.wait_ge(pv_done, n + 1)
                if t == 0 and b:
                    dve.wait_ge(m_full, M["attn", b - 1])
                ov = o_ps[:, 0:HEADS * VW].rearrange("p (h w) -> p h w", w=VW)
                do(dve.reciprocal(rsum[:], ov[:, :, HD]))
                dve.tensor_tensor(attn[:, t, :].rearrange("p (h w) -> p h w", w=HD), ov[:, :, 0:HD],
                                  rsum[:].unsqueeze(2).to_broadcast([P, HEADS, HD]), ALU.mult).then_inc(o_read, 1)

            do(dve.memset(carry[:], 0.0))
            stats1(0)
            dve.wait_ge(m_full, 1)
            dve.tensor_scalar(wT[:, 0:D], m_ps[:, 0:D], float(HD) ** -0.5, None, ALU.mult)
            spread = lambda w: w.rearrange("p (g r) -> p g r", g=GROUPS).unsqueeze(2).to_broadcast([P, GROUPS, 4, QD])
            dve.tensor_copy(wk_rep[:], spread(m_ps[:, D:2 * D]))
            dve.tensor_copy(wvT[:, 0:D], m_ps[:, 2 * D:3 * D])
            read_m(dve.tensor_copy(wT[:, D:], m_ps[:, 3 * D:]))
            misc("norm1", 0)
            dve.wait_ge(m_read, M["w", 0])
            dve.tensor_copy(wq_rep[:], spread(wT[:, 0:D])).then_inc(wq_done, 1)
            dve.wait_ge(ld_c, 32)
            misc("k", 0)
            stats1(1)
            for g in range(GROUPS):
                dve.wait_ge(f_copy, 3 + g)
                dve.scalar_tensor_tensor(q_rows[:, 0, g, :], q_parts[:, g % 2, :].bitcast(f32), C("qlow"), sc_ps[:, g, :],
                                         ALU.mult, ALU.add).then_inc(f_rows, 1)
            dve.wait_ge(set_p, 3)
            for b in range(B):
                last = dve.tensor_copy(vblk[:, b, :, 0:CHEADS * VW].rearrange("p c (h w) -> p c h w", w=VW)[:, :, :, HD],
                                       C("vmask").rearrange("p (c h) -> p c h", c=CH))
            do(last)
            softmax(0)
            misc("v", 0)
            misc("norm1", 1)
            dve.tensor_copy(upper_b[:], C("upper"))
            do(dve.tensor_copy(ones_b[:], C("ones")))

            def slot_of(n, k):
                for step in slot_steps(n, k):
                    misc(*step)

            for n in range(TILES):
                slot_of(n, 0)
                if n + 1 < TILES:
                    softmax(n + 1)
                slot_of(n, 1)
                normalise(n)
                slot_of(n, 2)
            for step in FINISH:
                misc(*step)
            dve.tensor_copy(carryb[:], carry[:]).then_inc(cast_done, 1)
            dve.wait_ge(m_full, M["count", 0])
            cnt = m_ps[:, 0:E]
            dve.tensor_tensor(tbi[:, 2, :], cnt, C("ebase"), ALU.add).then_inc(counts_done, 1)
            do(dve.tensor_scalar(tbi[:, 0, :], cnt, float(P - 1), None, ALU.add))
            do(dve.tensor_single_scalar(tbi[:, 1, :], tbi[:, 0, :], 7, ALU.logical_shift_right))
            do(dve.tensor_copy(tb[:, 0, :], tbi[:, 1, :]))
            do(dve.tensor_tensor(cmp[:, 0, 0:E * E].rearrange("p (a b) -> p a b", a=E), C("le").rearrange("p (a b) -> p a b", a=E),
                                 tb[:, 0, :].unsqueeze(1).to_broadcast([P, E, E]), ALU.mult))
            do(dve.tensor_reduce(tb[:, 1, :], cmp[:, 0, 0:E * E].rearrange("p (a b) -> p a b", a=E), AX, ALU.add))
            je = lambda a: a.rearrange("p (j e) -> p j e", e=E)
            jb = lambda a: a.unsqueeze(1).to_broadcast([P, NT, E])
            do(dve.tensor_tensor(je(cmp[:, 1, :]), jb(tb[:, 1, :]), je(C("tile")), ALU.is_le))
            do(dve.tensor_tensor(je(cmp[:, 2, :]), je(cmp[:, 1, :]), jb(tb[:, 0, :]), ALU.mult))
            do(dve.tensor_reduce(tj[:, 0, :], je(cmp[:, 1, :]), AX, ALU.add))
            do(dve.tensor_reduce(tj[:, 1, :], je(cmp[:, 2, :]), AX, ALU.add))
            do(dve.scalar_tensor_tensor(tj[:, 2, :], tj[:, 1, :], -float(P), C("tile128"), ALU.mult, ALU.add))
            do(dve.scalar_tensor_tensor(tj[:, 3, :], tj[:, 0, :], float(REG), tj[:, 2, :], ALU.mult, ALU.add))
            dve.tensor_scalar(first_row[:], tj[:, 3, :], float(PADROW), None, ALU.min)
            dve.tensor_scalar(tile_expert[:], tj[:, 0, :], float(E - 1), None, ALU.min).then_inc(tab_done, 1)
            dve.wait_ge(exp_w, 1)
            do(dve.tensor_scalar(wts[:, 1, :], wts[:, 0, :], 1.0, None, ALU.add))
            do(dve.reciprocal(wts[:, 1, :], wts[:, 1, :]))
            do(dve.tensor_scalar(wts[:, 2, :], wts[:, 1, :], tg[:, 1:2], None, ALU.mult))
            dve.tensor_tensor(wts[:, 3, :], wts[:, 0, :], wts[:, 2, :], ALU.mult).then_inc(wts_done, 1)
            dve.wait_ge(tab_done, 1)
            dve.wait_ge(ld_e, 16 * (2 + KF))

            def weights(i, c, ex):
                j, u, r, w = tile(i, c)
                if c >= U:
                    dve.wait_ge(h_done, j - U + 1)
                dve.tensor_copy(w1_now[:, u:u + 1, :], w1_sb[:, ds(ex, 1), :]).then_inc(w1_ready, 1)

            def result(i, c, ex):
                j, u, r, w = tile(i, c)
                dve.wait_ge(dn_full, j + 1)
                if c >= R:
                    dve.wait_ge(y_out[r], 16 * w)
                dve.tensor_tensor(yt[:, r, :].unsqueeze(1), y_ps.unsqueeze(1), b2_bc[:, ds(ex, 1), :], ALU.add).then_inc(y_done, 1)

            def step(i, c, ex, ahead):
                weights(i, c + 2, ahead)
                result(i, c, ex)

            ex = load_experts(DVE, 0, 0, R + 2)
            weights(0, 0, ex[0])
            weights(0, 1, ex[1])
            for c in range(R):
                step(0, c, ex[c], ex[c + 2])
            with dve.Fori(0, NT // R - 1) as i:
                ex = load_experts(DVE, i, R, R + 2)
                for c in range(R, 2 * R):
                    step(i, c, ex[c - R], ex[c - R + 2])
            i = NT // R - 1
            ex = load_experts(DVE, i, R, NT % R)
            for c in range(NT % R - 2):
                step(i, R + c, ex[c], ex[c + 2])
            for c in range(NT % R - 2, NT % R):
                result(i, R + c, ex[c])
            for b in range(B):
                dve.wait_ge(ld_y[b], 16)
                for t in range(T):
                    n = T * b + t
                    last = dve.scalar_tensor_tensor(acc[:, n, :], yy[:, b, t, 0:D], wts[:, 2, n:n + 1], x1[:, n, :], ALU.mult, ALU.add)
                do(last)
                dve.wait_ge(second_done, b + 1)
                dve.tensor_tensor(res[:, T * b:T * b + T, :], acc[:, T * b:T * b + T, :], second[:, T * b:T * b + T, :], ALU.add).then_inc(res_done, 1)

        @block.gpsimd
        def _(pool):
            pool.memset(wvT[:, D:], 0.0).then_inc(set_p, 1)
            pool.memset(wg_sb[:, E:], 0.0).then_inc(set_p, 1)
            pool.memset(vblk[:], 0.0).then_inc(set_p, 1)
            steps = [0]

            def done(ins):
                steps[0] += 1
                ins.then_inc(p_step, 1)
                pool.wait_ge(p_step, steps[0])

            def k_block(b):
                pool.wait_ge(m_read, M["k", b])
                pool.tensor_tensor(kblk[:, b, :].rearrange("p (g h k) -> p g h k", g=GROUPS, k=KEYS),
                                   k_rows[:].bitcast(f32).rearrange("p (g k) -> p g k", g=GROUPS).unsqueeze(2).to_broadcast([P, GROUPS, GRP, KEYS]),
                                   C("kmask").unsqueeze(1).unsqueeze(3).to_broadcast([P, GROUPS, GRP, KEYS]), ALU.mult).then_inc(k_done, 1)

            def newton_root(b, seeded, half, rs, rooted):
                pool.wait_ge(seeded, b + 1)
                h, y = half[:, T * b:T * b + T], rs[:, T * b:T * b + T]
                for k in range(3):
                    done(pool.tensor_tensor(newton[:], y, y, ALU.mult))
                    done(pool.tensor_tensor(newton[:], newton[:], h, ALU.mult))
                    done(pool.tensor_scalar(newton[:], newton[:], 1.5, None, ALU.add))
                    last = pool.tensor_tensor(y, y, newton[:], ALU.mult)
                    if k < 2:
                        done(last)
                last.then_inc(rooted, 1)
                pool.wait_ge(rooted, b + 1)

            def with_bias(b):
                pool.wait_ge(ld_x[b], 16)
                pool.tensor_tensor(xb[:, T * b:T * b + T, :], x_sb[:, T * b:T * b + T, :],
                                   tbo[:].unsqueeze(1).to_broadcast([P, T, D]), ALU.add).then_inc(xb_done, 1)

            def put_ids(to, ts, al):
                for k in range(2):
                    last = pool.tensor_copy(to[:, k, ts, D:ROWW].bitcast(i32),
                                            cint[:, 2 * al.start:2 * al.stop].rearrange("p (t k) -> p t k", k=2)[:, :, k:k + 1])
                return last

            def prepare(g):
                ts, al = at_parcel(g)
                pool.wait_ge(xs_done, g + 1)
                if g:
                    pool.wait_ge(*sent(freed(g)))
                for k in range(2):
                    pool.tensor_copy(rows[:, k, ts, 0:D], xs[:, ts, :])
                put_ids(rows, ts, al).then_inc(rows_done, 1)

            def send(g, k):
                ts, _ = at_parcel(g)
                pool.wait_ge(slots_done, g + 1)
                if g < B - 1:
                    source, place = rows, slot
                    pool.wait_ge(rows_done, g + 1)
                else:
                    source, place = rows_last, slot_last
                    pool.wait_ge(rows_last_done, g - B + 2)
                    pool.wait_ge(ids_last, 1)
                for t in range(ts.start, ts.stop):
                    pool.indirect_dma_start(out=rows_dram, out_offset=bass.IndirectOffsetOnAxis(ap=place[:, k, t:t + 1], axis=0),
                                            in_=source[:, k, t, :], in_offset=None, bounds_check=PADROW + P - 1,
                                            oob_is_err=False).then_inc(scat[g % 2], 16)

            newton_root(0, seed1, half1, rs1, root1)
            pool.wait_ge(ld_c, 32)
            k_block(0)
            newton_root(1, seed1, half1, rs1, root1)
            pool.wait_ge(tanh_done, 1)
            done(pool.tensor_scalar(tbo[:], bo[:], tg[:, 0:1], None, ALU.mult))
            pool.wait_ge(m_read, M["w", 0])
            pool.tensor_scalar(wT[:, D:], wT[:, D:], tg[:, 0:1], None, ALU.mult).then_inc(wout_done, 1)
            put_ids(rows_last, slice(0, T), slice(TILES - T, TILES)).then_inc(ids_last, 1)
            for b in range(B):
                with_bias(b)
            k_block(1)
            newton_root(2, seed1, half1, rs1, root1)
            for b in range(1, B):
                if b + 2 < B:
                    newton_root(b + 2, seed1, half1, rs1, root1)
                if b > 1:
                    send(b - 2, 0)
                if b + 1 < B:
                    k_block(b + 1)
                newton_root(b - 1, seed2, half2, rs2, root2)
                if b > 1:
                    send(b - 2, 1)
                prepare(b - 1)
            for k in range(2):
                send(B - 2, k)
            for g in range(B - 1, len(PARCELS)):
                for k in range(2):
                    send(g, k)
            pool.wait_ge(tab_done, 1)

            def ids(i, c):
                j, u, r, w = tile(i, c)
                pool.wait_ge(x_tile[r], 16 * (w + 1))
                if c >= R:
                    pool.wait_ge(y_out[r], 16 * w)
                at = xg[:, r, D:ROWW].bitcast(i32)
                pool.tensor_tensor(dest[:, r:r + 1], at, cint[:, 2 * TILES:2 * TILES + 1], ALU.add).then_inc(id_done, 1)

            def y_send(i, c):
                j, u, r, w = tile(i, c)
                n = j + 1 if isinstance(i, int) else pool.snap(j + 1)
                pool.wait_ge(id_done, n)
                pool.wait_ge(y_done, n)
                pool.reg_add(bound, last, 1)
                pool.indirect_dma_start(out=y_dram, out_offset=bass.IndirectOffsetOnAxis(ap=dest[:, r:r + 1], axis=0),
                                        in_=yt[:, r, :], in_offset=None, bounds_check=bound, oob_is_err=False).then_inc(y_out[r], 16)

            last, bound = pool.alloc_register("last_result"), pool.alloc_register("bound")
            pool.reg_mov(last, 2 * TOK - 2)
            ids(0, 0)
            for c in range(R - 1):
                ids(0, c + 1)
                y_send(0, c)
            with pool.Fori(0, NT // R - 1) as i:
                for c in range(R - 1, 2 * R - 1):
                    ids(i, c + 1)
                    y_send(i, c)
            i = NT // R - 1
            for c in range(R - 1, NT - R * i - 1):
                ids(i, c + 1)
                y_send(i, c)
            y_send(i, NT - R * i - 1)


_INS = ["x", "ctx_1024", "g_xattn", "g_ffn", "L0_xattn_Wq", "L0_xattn_Wkv", "L0_xattn_Wout", "L0_xattn_bout",
        "L0_ffn_Wg", "L0_ffn_W1", "L0_ffn_b1", "L0_ffn_W2", "L0_ffn_b2"]
_OUTS = [((B, S, D), "float32")]


def kernel(**inputs):
    import numpy as _np
    import concourse.bacc as _bacc
    from concourse import mybir as _mybir
    from concourse.bass_utils import run_bass_kernel_spmd as _run

    nc = _bacc.Bacc("TRN2", target_bir_lowering=False, num_devices=1)
    arrays, args = {}, []
    given = [(n, _np.ascontiguousarray(inputs[n])) for n in _INS]
    for name, a in given + list(zip(("constants", "integers"), constants())):
        arrays[f"in_{name}_dram"] = a
        args.append(nc.dram_tensor(f"in_{name}_dram", a.shape, _mybir.dt.from_np(a.dtype), kind="ExternalInput").ap())
    for i, (shape, dtype) in enumerate(_OUTS):
        dt = _mybir.dt.from_np(_np.dtype(dtype))
        args.append(nc.dram_tensor(f"out_{i}_dram", shape, dt, kind="ExternalOutput").ap())
    flamingo(nc, *args)
    r = _run(nc, [arrays], core_ids=[0])
    return r.results[0]["out_0_dram"]
```
